# Optimizing a Trainium2 kernel written in Bass

```python
import numpy as np
import jax
import jax.numpy as jnp

def _softmax(x, axis=-1):
    return jax.nn.softmax(x, axis=axis)

def _gelu(x):
    return jax.nn.gelu(x, approximate=True)

def _silu(x):
    return jax.nn.silu(x)

def _sigmoid(x):
    return jax.nn.sigmoid(x)

def _layernorm(x, axis=-1, eps=1e-05):
    m = jnp.mean(x, axis=axis, keepdims=True)
    v = jnp.var(x, axis=axis, keepdims=True)
    return (x - m) / jnp.sqrt(v + eps)

def _scatter_add(tgt, idx, src, axis=0):
    return tgt.at[idx].add(src)

def _segment_sum(src, seg, n):
    return jax.ops.segment_sum(src, seg, n)
kernel_name = 'mk_seq_preln_d1_jaxref_r4_37a244'

def setup_inputs(seed: int=0):
    np.random.seed(seed)
    _w = jnp.asarray

    def _L0_attn_setup():
        import jax, jax.numpy as jnp
        import numpy as np
        EPS = 1e-06

        def _feature_map(x):
            return jax.nn.elu(x) + 1.0
        key = jax.random.key(seed)
        ks = jax.random.split(key, 4)
        B, L, C = (4, 2048, 256)
        s = 1.0 / np.sqrt(C)
        x = jax.random.normal(ks[0], (B, L, C), dtype=jnp.float32)
        Wq = jax.random.normal(ks[1], (C, C), dtype=jnp.float32) * s
        Wk = jax.random.normal(ks[2], (C, C), dtype=jnp.float32) * s
        Wv = jax.random.normal(ks[3], (C, C), dtype=jnp.float32) * s
        bq = jnp.zeros((C,), jnp.float32)
        bk = jnp.zeros((C,), jnp.float32)
        bv = jnp.zeros((C,), jnp.float32)
        return {'x': x, 'Wq': Wq, 'bq': bq, 'Wk': Wk, 'bk': bk, 'Wv': Wv, 'bv': bv}
    _L0_attn_in = _L0_attn_setup()

    def _L0_ffn_setup():
        import jax, jax.numpy as jnp
        import numpy as np
        D_MODEL = 256
        NUM_EXPERTS = 8
        HIDDEN = 1024
        TOP_K = 2
        key = jax.random.key(seed)
        ks = jax.random.split(key, 6)
        x = jax.random.normal(ks[0], (2, 256, D_MODEL), dtype=jnp.float32)
        gate_w = jax.random.normal(ks[1], (NUM_EXPERTS, D_MODEL), dtype=jnp.float32) * (1.0 / np.sqrt(D_MODEL))
        w1 = jax.random.normal(ks[2], (NUM_EXPERTS, HIDDEN, D_MODEL), dtype=jnp.float32) * (1.0 / np.sqrt(D_MODEL))
        b1 = jax.random.normal(ks[3], (NUM_EXPERTS, HIDDEN), dtype=jnp.float32) * 0.01
        w2 = jax.random.normal(ks[4], (NUM_EXPERTS, D_MODEL, HIDDEN), dtype=jnp.float32) * (1.0 / np.sqrt(HIDDEN))
        b2 = jax.random.normal(ks[5], (NUM_EXPERTS, D_MODEL), dtype=jnp.float32) * 0.01
        return {'x': x, 'gate_w': gate_w, 'w1': w1, 'b1': b1, 'w2': w2, 'b2': b2}
    _L0_ffn_in = _L0_ffn_setup()
    _d = {'L0_attn_x': _L0_attn_in['x'], 'L0_attn_Wq': _L0_attn_in['Wq'], 'L0_attn_bq': _L0_attn_in['bq'], 'L0_attn_Wk': _L0_attn_in['Wk'], 'L0_attn_bk': _L0_attn_in['bk'], 'L0_attn_Wv': _L0_attn_in['Wv'], 'L0_attn_bv': _L0_attn_in['bv'], 'L0_ffn_gate_w': _L0_ffn_in['gate_w'], 'L0_ffn_w1': _L0_ffn_in['w1'], 'L0_ffn_b1': _L0_ffn_in['b1'], 'L0_ffn_w2': _L0_ffn_in['w2'], 'L0_ffn_b2': _L0_ffn_in['b2']}
    _x0 = _d['L0_attn_x']
    _d['L0_attn_x'] = jax.random.normal(jax.random.fold_in(jax.random.key(seed), 1), (1, 4096, 256), dtype=_x0.dtype)
    del _x0
    return _d

def reference(L0_attn_x, L0_attn_Wq, L0_attn_bq, L0_attn_Wk, L0_attn_bk, L0_attn_Wv, L0_attn_bv, L0_ffn_gate_w, L0_ffn_w1, L0_ffn_b1, L0_ffn_w2, L0_ffn_b2):

    def _L0_attn_ref(x, Wq, bq, Wk, bk, Wv, bv):
        import jax, jax.numpy as jnp
        import numpy as np
        EPS = 1e-06

        def _feature_map(x):
            return jax.nn.elu(x) + 1.0
        B, L, C = x.shape
        H = 8
        D = C // H
        q = x @ Wq + bq
        k = x @ Wk + bk
        v = x @ Wv + bv
        q = q.reshape(B, L, H, D)
        k = k.reshape(B, L, H, D)
        v = v.reshape(B, L, H, D)
        Q = _feature_map(q)
        K = _feature_map(k)
        v_len = jnp.asarray(L, v.dtype)
        v_scaled = v / v_len
        KV = jnp.einsum('nshd,nshv->nhdv', K, v_scaled)
        Z = 1.0 / (jnp.einsum('nlhd,nhd->nlh', Q, K.sum(axis=1)) + EPS)
        out = jnp.einsum('nlhd,nhdv,nlh->nlhv', Q, KV, Z) * v_len
        return out.reshape(B, L, C)

    def _L0_ffn_ref(x, gate_w, w1, b1, w2, b2):
        import jax, jax.numpy as jnp
        import numpy as np
        D_MODEL = 256
        NUM_EXPERTS = 8
        HIDDEN = 1024
        TOP_K = 2
        B, S, D = x.shape
        xf = x.reshape(-1, D)
        T = xf.shape[0]
        gate_logits = xf @ gate_w.T
        gate_probs = jax.nn.softmax(gate_logits, axis=-1)
        topk_scores, topk_idx = jax.lax.top_k(gate_probs, TOP_K)
        topk_scores = topk_scores / jnp.sum(topk_scores, axis=-1, keepdims=True)
        combine = jnp.zeros((T, NUM_EXPERTS), dtype=x.dtype)
        combine = combine.at[jnp.arange(T)[:, None], topk_idx].set(topk_scores)
        h = jax.nn.relu(jnp.einsum('td,ehd->teh', xf, w1) + b1)
        expert_out = jnp.einsum('teh,edh->ted', h, w2) + b2
        out = jnp.einsum('ted,te->td', expert_out, combine)
        return out.reshape(B, S, D)
    x = L0_attn_x
    x = x + _L0_attn_ref(_layernorm(x, axis=-1), L0_attn_Wq, L0_attn_bq, L0_attn_Wk, L0_attn_bk, L0_attn_Wv, L0_attn_bv)
    x = x + _L0_ffn_ref(_layernorm(x, axis=-1), L0_ffn_gate_w, L0_ffn_w1, L0_ffn_b1, L0_ffn_w2, L0_ffn_b2)
    return x

_drawn_inputs = setup_inputs


def setup_inputs(seed=0):
    import zlib

    import numpy as np

    out = dict(_drawn_inputs(seed))
    spreads = {'L0_attn_bq': (0.0, 0.8), 'L0_attn_bk': (0.0, 0.8), 'L0_attn_bv': (0.0, 0.1)}
    factors = {'L0_attn_Wq': 2.801, 'L0_ffn_b1': 8.0, 'L0_ffn_b2': 8.0}
    for name, (base, spread) in spreads.items():
        noise = np.random.default_rng([zlib.crc32(name.encode()), seed]).standard_normal(out[name].shape)
        drawn = base * np.exp(spread * noise) if base else spread * noise
        out[name] = jnp.asarray(drawn.astype(out[name].dtype))
    for name, factor in factors.items():
        out[name] = (out[name] * factor).astype(out[name].dtype)
    return out
```

```python
from contextlib import ExitStack

import concourse.bass as bass
from concourse import mybir

ALU = mybir.AluOpType
ACT = mybir.ActivationFunctionType
AX = mybir.AxisListType
F32 = mybir.dt.float32
F16 = mybir.dt.float16
I32 = mybir.dt.int32
RMAX = bass.bass_isa.ReduceOp.max

P = 128
GT = 4
LN_EPS = 1e-5
ATT_EPS = 1e-6
ZBOUND = 16.0
ZSCALE = 1024.0
TOP = 2.0 ** 14
TINY = 1e-12


def dyn(i, n=1):
    return bass.DynSlice(i, n)


def staged(eng, n, steps):
    lags = max(lag for _, lag in steps)

    def slot(i, u, number=None):
        for f, lag in steps:
            if number is None or lag <= number < n + lag:
                f(i - (lag + 1 - u) // 2, (u + lag) % 2)
    for k in range(4):
        slot(k // 2, k % 2, k)
    with eng.Fori(2, n // 2) as i:
        slot(i, 0)
        slot(i, 1)
    for k in range(n // 2 * 2, n + lags):
        slot(k // 2, k % 2, k)


def attention_moe(nc, x, wq, bq, wk, bk, wv, bv, gate_w, w1, b1, w2, b2, out):
    T, C = x.shape
    E = gate_w.shape[2]
    HC = b1.shape[2]
    CC = C // P
    NH = 8
    D = C // NH
    HB = P // D
    NG = T // (GT * P)
    TS = 2 * P
    NT = (2 * T + E * (TS - 1)) // TS
    CAP = T + TS
    SPARE = NT - 2 * T // TS
    ROW = C + 16
    COMB, TOK = C, C + E
    VW = D + 1
    NHC = HB * VW
    PIECE = HC * C
    assert 2 * E == 2 * NG and NG % 2 == 0

    scratch = nc.dram_tensor("rows_by_expert", [E * CAP + SPARE * TS, ROW], I32, kind="Internal").ap()
    qt_dram = nc.dram_tensor("q_transposed", [NG, P, CC * GT * P], F32, kind="Internal").ap()
    x_v = x.rearrange("(g p j) c -> g p (j c)", p=P, j=GT)
    out_v = out.rearrange("(g p j) c -> g p (j c)", p=P, j=GT)

    with ExitStack() as ctx:
        def sb(name, shape, dt=F32, scope=ctx):
            return scope.enter_context(nc.sbuf_tensor(name, shape, dt))

        def sem(name):
            return ctx.enter_context(nc.semaphore(name))

        ps = ctx.enter_context(nc.psum_tensor("ps", [P, 8, 512], F32))
        w1s = sb("w1_split", [P, E, 2, PIECE], F16)
        w2s = sb("w2_split", [P, E, HC, 2, C], F16)
        ident = sb("ident", [P, P])
        tri = sb("tri", [P, P], F16)
        ones = sb("ones", [P, P], F16)
        ident16 = sb("ident16", [P, P], F16)
        wkv_sb = sb("wkv_sb", [P, CC, 2, C])
        bq_sb = sb("bq_sb", [P, CC])
        gw_sb = sb("gw_sb", [P, CC, E])
        b1_sb = sb("b1_sb", [P, E, HC])
        b1s = sb("b1_scaled", [P, E, HC])
        kv_bd = sb("kv_blockdiag", [P, CC, NHC])
        pad = sb("pad_rows", [P, 2, ROW], I32)
        tok_ids = sb("tok_ids", [P, NG, GT], I32)
        wmax = sb("wmax", [P, E, 2])
        winv = sb("winv", [P, E, 2])
        b1max = sb("b1max", [P, E])
        b1maxr = sb("b1maxr", [P, E])
        hscale = sb("hscale", [P, E])
        hinv = sb("hinv", [P, E])
        htmp = sb("htmp", [P, 2, E])
        l1_scale = sb("l1_scale", [P, E])
        y_scale = sb("y_scale", [P, E])
        am = sb("am", [P, 2])
        amr = sb("amr", [P, 2])
        wt = sb("wt", [P, 2])
        wsc = sb("wsc", [P, 2])
        rev_i = sb("rev_i", [P, GT, E], I32)
        rev = sb("rev", [P, GT, E])
        base_i = sb("base_i", [P, E], I32)
        base = sb("base", [P, E])
        start_row = sb("start_row", [P, E])
        tiles_i = sb("tiles_i", [1, NT], I32)
        tile_no = sb("tile_no", [1, NT])
        low_i = sb("low_i", [1, E, E], I32)
        low = sb("low", [1, E, E])
        cnt_i = sb("cnt_i", [1, 2, E], I32)
        ntile = sb("ntile", [1, E])
        ends = sb("ends", [1, E])
        ends3 = sb("ends3", [1, E, E])
        past = sb("past", [1, NT, E])
        past_n = sb("past_n", [1, NT, E])
        tab_f = sb("tab_f", [1, 4, NT])
        pad_row = sb("pad_row", [1, E], I32)
        tile_row = sb("tile_row", [1, NT], I32)
        tile_exp = sb("tile_exp", [1, NT], I32)

        s12 = ExitStack()
        xr = sb("x_ring", [P, 2, GT, C], scope=s12)
        qt = sb("qt_ring", [P, 2, CC, GT * P], scope=s12)
        stage = sb("w_stage", [P, 2, PIECE], scope=s12)
        st = sb("bn_st", [P, GT, 6], scope=s12)
        mv = sb("mean_var", [P, GT, 2], scope=s12)
        rstd = sb("rstd", [P, GT], scope=s12)
        ve = sb("ve", [P, GT], scope=s12)
        half = sb("half", [P, GT], I32, scope=s12)
        nt = sb("newton", [P, 2, GT], scope=s12)
        zT = sb("zT", [P, 2, CC, GT * P], scope=s12)
        s1 = ExitStack()
        wq_sb = sb("wq_sb", [P, CC, C], scope=s1)
        bkv_sb = sb("bkv_sb", [P, 2 * NH, D], scope=s1)
        z = sb("z", [P, GT, C], scope=s1)
        kv = sb("kv", [P, GT, 2 * NH, VW], scope=s1)
        kf = sb("kf", [P, GT, C], scope=s1)
        kexp = sb("kexp", [P, 2, C], scope=s1)
        qrelu = sb("qrelu", [P, GT * P], scope=s1)
        s1.close()
        x2 = sb("x2", [P, GT, C], scope=s12)
        z2 = sb("z2", [P, 2, GT, C], scope=s12)
        rows = sb("rows", [P, 2, GT, ROW], I32, scope=s12)
        den = sb("den", [P, GT, NH], scope=s12)
        rden = sb("rden", [P, GT, NH], scope=s12)
        lg = sb("lg", [P, GT, E], scope=s12)
        lg2 = sb("lg2", [P, GT, E], scope=s12)
        eq = sb("eq", [P, GT, E], scope=s12)
        cand = sb("cand", [P, GT, E], scope=s12)
        mx = sb("mx", [P, 2, GT], scope=s12)
        first = sb("first", [P, GT], scope=s12)
        m1 = sb("m1", [P, GT, E], scope=s12)
        m2 = sb("m2", [P, GT, E], scope=s12)
        msum = sb("msum", [P, GT + 1, E], F16, scope=s12)
        wts = sb("wts", [P, 5, GT], scope=s12)
        cb = sb("cb", [P, 2, GT, E], scope=s12)
        pos = sb("pos", [P, GT, E], scope=s12)
        pos1 = sb("pos1", [P, GT, E], scope=s12)
        idx = sb("idx", [P, 2, 2, GT], I32, scope=s12)
        s12.close()
        rin = sb("rin", [P, 2, 2, ROW], I32)
        zin = sb("zin", [P, 2, 2 * CC, TS], F16)
        meta = sb("meta", [P, 2, 2, 16], I32)
        hx = sb("hx", [P, 4, 512])
        hhi = sb("hhi", [P, 2, HC, TS], F16)
        hlo = sb("hlo", [P, 2, HC, TS], F16)
        b2_sb = sb("b2_sb", [P, E, C])
        yu = sb("yu", [P, 2, C])
        yv = sb("yv", [P, 2, C])
        y = sb("y", [P, 2, 2, C])

        names = """consts kv_ones pad_out spare_out b2_in
            stats1 aggr1 rstd1 z1 zt_psum zt_sb q_psum q_act q_done kv_psum kv_biased k_act k_done kv_sum
            kvbd wabs wabs_all wscale_s wscale whi wlo
            num_psum dens rdens att x2_done stats2 aggr2 rstd2 z2_done z2t_psum z2t_sb zhi row_data
            logit_psum gate_steps gap_exp rank_psum placed pl_steps scattered
            h_steps b1_all tab_steps tables pads_out
            l1_psum hx_done hi_done lo_done l2_psum yu_done yv_done y_done added""".split()
        s = {n: sem(n) for n in names}
        (consts, kv_ones, pad_out, spare_out, b2_in,
         stats1, aggr1, rstd1, z1, zt_psum, zt_sb, q_psum, q_act, q_done, kv_psum, kv_biased, k_act,
         k_done, kv_sum, kvbd, wabs, wabs_all, wscale_s, wscale, whi, wlo,
         num_psum, dens, rdens, att, x2_done, stats2, aggr2, rstd2, z2_done, z2t_psum, z2t_sb, zhi,
         row_data, logit_psum, gate_steps, gap_exp, rank_psum, placed, pl_steps, scattered,
         h_steps, b1_all, tab_steps, tables, pads_out,
         l1_psum, hx_done, hi_done, lo_done, l2_psum, yu_done, yv_done, y_done, added) = (s[n] for n in names)
        params_in = sem("params_in")
        x_in = [sem("x_in0"), sem("x_in1")]
        w_in = [sem("w_in0"), sem("w_in1")]
        qt_out = [sem("qt_out0"), sem("qt_out1")]
        qt_in = [sem("qt_in0"), sem("qt_in1")]
        x2_out = sem("x2_out")
        rows_in = [sem("rows_in0"), sem("rows_in1")]
        zin_psum, zin_sb, meta_done = sem("zin_psum"), sem("zin_sb"), sem("meta_done")
        NPARAM = 8
        NCONST = 9
        pool_go, dve_go = sem("pool_go"), sem("dve_go")

        RSTEPS = 12
        GS, GAP_AT = 21, 12
        ctx.enter_context(nc.allow_low_precision(reason="row numbers, summed in float32 into int32, are exact"))
        block = ctx.enter_context(nc.Block())

        @block.sync
        def _(sp):
            def load_w(i, kind):
                src = (w1 if kind == 0 else w2)[dyn(i)].rearrange("a p n -> p (a n)")
                sp.dma_start(stage[:, kind], src).then_inc(w_in[kind], 16)

            sp.dma_start(xr[:, 0].rearrange("p j c -> p (j c)"), x_v[0]).then_inc(x_in[0], 16)
            sp.dma_start(wkv_sb[:, :, 0], wk).then_inc(params_in, 16)
            sp.dma_start(wkv_sb[:, :, 1], wv).then_inc(params_in, 16)
            sp.dma_start(bkv_sb[:, 0:NH].rearrange("p h d -> p (h d)"), bk.partition_broadcast(P)).then_inc(params_in, 16)
            sp.dma_start(bkv_sb[:, NH:].rearrange("p h d -> p (h d)"), bv.partition_broadcast(P)).then_inc(params_in, 16)
            sp.dma_start(wq_sb[:], wq).then_inc(params_in, 16)
            sp.dma_start(bq_sb[:], bq).then_inc(params_in, 16)
            sp.dma_start(gw_sb[:], gate_w).then_inc(params_in, 16)
            sp.dma_start(b1_sb[:], b1).then_inc(params_in, 16)
            load_w(0, 0)
            sp.dma_start(xr[:, 1].rearrange("p j c -> p (j c)"), x_v[1]).then_inc(x_in[1], 16)
            load_w(0, 1)
            sp.wait_ge(pad_out, 3)
            for k in range(SPARE):
                lo = E * CAP + k * TS
                sp.dma_start(scratch[lo:lo + TS].rearrange("(p s) r -> p (s r)", p=P),
                             pad[:].rearrange("p s r -> p (s r)")).then_inc(spare_out, 16)

            def store_q(i, u):
                sp.wait_ge(q_done, CC * (2 * i + u + 1))
                sp.dma_start(qt_dram[dyn(2 * i + u)].rearrange("a p n -> p (a n)"),
                             qt[:, u].rearrange("p c n -> p (c n)")).then_inc(qt_out[u], 16)

            store_q(0, 0)
            with sp.Fori(1, NG // 2) as i:
                for u in range(2):
                    sp.wait_ge(z1, GT * (2 * i + u - 1))
                    sp.dma_start(xr[:, u].rearrange("p j c -> p (j c)"),
                                 x_v[dyn(2 * i + u)].rearrange("a p n -> p (a n)")).then_inc(x_in[u], 16)
                    sp.wait_ge(wlo, 2 * i + u - 1)
                    load_w(i, u)
                    store_q(i if u else i - 1, 1 - u)
            store_q(NG // 2 - 1, 1)

            H2 = NG // 2

            def load2(i, u):
                g = 2 * i + u
                if isinstance(i, int) and i == 0:
                    sp.wait_ge(z1, GT * (NG - 1 + u))
                else:
                    sp.wait_ge(x2_done, g - 1)
                sp.dma_start(xr[:, u].rearrange("p j c -> p (j c)"),
                             x_v[dyn(g)].rearrange("a p n -> p (a n)")).then_inc(x_in[u], 16)
                sp.wait_ge(qt_out[u], 16 * H2)
                if not (isinstance(i, int) and i == 0):
                    sp.wait_ge(num_psum, GT * (g - 1))
                sp.dma_start(qt[:, u].rearrange("p c n -> p (c n)"),
                             qt_dram[dyn(g)].rearrange("a p n -> p (a n)")).then_inc(qt_in[u], 16)
                sp.wait_ge(wlo, NG + g - 1)
                load_w(i + H2, u)

            def store_x2(i, u):
                sp.wait_ge(x2_done, 2 * i + u + 1)
                sp.dma_start(out_v[dyn(2 * i + u)].rearrange("a p n -> p (a n)"),
                             x2[:].rearrange("p j c -> p (j c)")).then_inc(x2_out, 16)

            staged(sp, NG, [(load2, 0), (store_x2, 1)])

            sp.wait_ge(placed, NG)
            sp.wait_ge(wlo, 2 * NG)
            sp.wait_ge(tables, 1)
            sp.wait_ge(x2_out, 16 * NG)
            sp.wait_ge(scattered, 16 * 2 * GT * NG)
            for e in range(E):
                r = sp.value_load(pad_row[0:1, e:e + 1], min_val=0, max_val=E * CAP - TS)
                sp.dma_start(scratch[dyn(r, TS)].rearrange("(p s) r -> p (s r)", p=P),
                             pad[:].rearrange("p s r -> p (s r)")).then_inc(pads_out, 16)
            sp.dma_start(b2_sb[:].rearrange("p e c -> p (e c)"), b2.partition_broadcast(P)).then_inc(b2_in, 16)
            sp.wait_ge(spare_out, 16 * SPARE)
            sp.wait_ge(pads_out, 16 * E)

            def load_rows(i, u):
                j = 2 * i + u
                r = sp.value_load(tile_row[0:1, dyn(j)], min_val=0, max_val=E * CAP + (SPARE - 1) * TS)
                if not (isinstance(i, int) and i == 0):
                    sp.wait_ge(meta_done, 2 * (j - 1))
                sp.dma_start(rin[:, u].rearrange("p h r -> p (h r)"),
                             scratch[dyn(r, TS)].rearrange("(p h) r -> p (h r)", p=P)).then_inc(rows_in[u], 16)

            staged(sp, NT, [(load_rows, 0)])

        @block.gpsimd
        def _(pool):
            g = nc.gpsimd
            g.memset(ident[:], 0.0).then_inc(consts, 1)
            g.memset(tri[:], 1.0).then_inc(consts, 1)
            g.memset(ones[:], 1.0).then_inc(consts, 1)
            pool.wait_ge(consts, 3)
            g.affine_select(out=ident[:], in_=ident[:], compare_op=ALU.not_equal, fill=1.0, base=0,
                            pattern=[[-1, P]], channel_multiplier=1).then_inc(consts, 1)
            g.affine_select(out=tri[:], in_=tri[:], compare_op=ALU.is_gt, fill=0.0, base=0,
                            pattern=[[1, P]], channel_multiplier=-1).then_inc(consts, 1)
            g.iota(rev_i[:], pattern=[[0, GT], [-1, E]], base=E, channel_multiplier=0).then_inc(consts, 1)
            g.iota(base_i[:], pattern=[[CAP, E]], base=0, channel_multiplier=0).then_inc(consts, 1)
            g.iota(tiles_i[:], pattern=[[1, NT]], base=0, channel_multiplier=0).then_inc(consts, 1)
            g.iota(low_i[:], pattern=[[1, E], [-1, E]], base=0, channel_multiplier=0).then_inc(consts, 1)
            g.iota(tok_ids[:], pattern=[[GT * P, NG], [1, GT]], base=0, channel_multiplier=GT).then_inc(pad_out, 1)

            def all_max(n, u):
                pool.wait_ge(wabs, n + 1)
                if not (isinstance(n, int) and n < 2):
                    pool.wait_ge(wscale, n - 1)
                pool.sem_inc(pool_go, 1)
                g.partition_all_reduce(amr[:, u:u + 1], am[:, u:u + 1], P, RMAX).then_inc(wabs_all, 1)

            def low_half(e, n, kind):
                pool.wait_ge(whi, 2 * (n + 1))
                if kind == 0:
                    hi, lo = w1s[:, dyn(e), 0].rearrange("p a n -> p (a n)"), w1s[:, dyn(e), 1].rearrange("p a n -> p (a n)")
                    g.tensor_tensor(lo, stage[:, 0], hi, ALU.subtract).then_inc(wlo, 1)
                else:
                    hi = w2s[:, dyn(e), :, 0].rearrange("p a h c -> p (a h) c")
                    lo = w2s[:, dyn(e), :, 1].rearrange("p a h c -> p (a h) c")
                    g.tensor_tensor(lo, stage[:, 1].rearrange("p (h c) -> p h c", h=HC), hi,
                                    ALU.subtract).then_inc(wlo, 1)

            staged(pool, NG, [(lambda i, u: all_max(2 * i + u, u), 0), (lambda i, u: low_half(i, 2 * i + u, u), 1)])
            pool.wait_ge(h_steps, 1)
            g.partition_all_reduce(b1maxr[:], b1max[:], P, RMAX).then_inc(b1_all, 1)

            def scatter(i, u):
                n = 2 * i + u
                pool.wait_ge(placed, n + 1)
                pool.wait_ge(row_data, 3 * (n + 1))
                pool.sem_inc(pool_go, 1)
                for j in range(GT):
                    for k in range(2):
                        g.indirect_dma_start(
                            out=scratch, out_offset=bass.IndirectOffsetOnAxis(ap=idx[:, u, k, j:j + 1], axis=0),
                            in_=rows[:, u, j], in_offset=None).then_inc(scattered, 16)

            staged(pool, NG, [(lambda i, u: all_max(NG + 2 * i + u, u), 0),
                              (lambda i, u: low_half(i + NG // 2, NG + 2 * i + u, u), 1), (scatter, 1)])

            pool.wait_ge(x2_out, 16 * NG)

            def add_rows(i, u):
                n = 2 * i + u
                for h in range(2):
                    pool.wait_ge(y_done, 2 * n + h + 1)
                    if not (isinstance(n, int) and n == 0 and h == 0):
                        pool.wait_ge(added, 16 * (2 * n + h))
                    pool.sem_inc(pool_go, 1)
                    g.indirect_dma_start(
                        out=out, out_offset=bass.IndirectOffsetOnAxis(ap=meta[:, u, h, E:E + 1], axis=0),
                        in_=y[:, u, h], in_offset=None, bounds_check=T - 1, oob_is_err=False,
                        compute_op=ALU.add).then_inc(added, 16)

            staged(pool, NT, [(add_rows, 0)])
            pool.wait_ge(added, 32 * NT)

        @block.scalar
        def _(act):
            a = nc.scalar

            def high_half(e, n, kind):
                act.wait_ge(wscale, n + 1)
                a.activation(stage[:, kind], stage[:, kind], ACT.Copy, scale=wsc[:, kind:kind + 1]).then_inc(whi, 1)
                act.wait_ge(whi, 2 * n + 1)
                if kind == 0:
                    a.activation(w1s[:, dyn(e), 0].rearrange("p a n -> p (a n)"), stage[:, 0], ACT.Copy).then_inc(whi, 1)
                else:
                    a.activation(w2s[:, dyn(e), :, 0].rearrange("p a h c -> p (a h) c"),
                                 stage[:, 1].rearrange("p (h c) -> p h c", h=HC), ACT.Copy).then_inc(whi, 1)

            def zt_copy(i, u):
                g = 2 * i + u
                act.wait_ge(zt_psum, g + 1)
                if not (isinstance(i, int) and i == 0):
                    act.wait_ge(kv_sum, GT * (g - 1))
                a.activation(zT[:, u], ps[:, 0:CC], ACT.Copy).then_inc(zt_sb, 1)

            def kq(i, u):
                g = 2 * i + u
                for j in range(GT):
                    n = GT * g + j
                    act.wait_ge(kv_biased, n + 1)
                    if not (isinstance(n, int) and n < 2):
                        act.wait_ge(k_done, n - 1)
                    kin = kv[:, j, 0:NH, 0:D]
                    a.activation(kexp[:, j % 2].rearrange("p (h d) -> p h d", h=NH), kin, ACT.Exp).then_inc(k_act, 1)
                    if not (isinstance(g, int) and g == 0):
                        act.wait_ge(kv_sum, n - GT + 1)
                    a.activation(kf[:, j].rearrange("p (h d) -> p h d", h=NH), kin, ACT.Relu).then_inc(k_act, 1)
                if not (isinstance(i, int) and i == 0):
                    act.wait_ge(qt_out[u], 16 * i)
                for f in range(CC):
                    act.wait_ge(q_psum, CC * g + f + 1)
                    if not (isinstance(g, int) and g == 0 and f == 0):
                        act.wait_ge(q_done, CC * g + f)
                    a.activation(qt[:, u, f], ps[:, 6 + f], ACT.Exp, bias=bq_sb[:, f:f + 1]).then_inc(q_act, 1)
                    a.activation(qrelu[:], ps[:, 6 + f], ACT.Relu, bias=bq_sb[:, f:f + 1]).then_inc(q_act, 1)

            act.wait_ge(params_in, 16 * NPARAM)
            staged(act, NG, [(kq, 1), (zt_copy, 0), (lambda i, u: high_half(i, 2 * i + u, u), 0)])

            def z2_side(i, u):
                g = 2 * i + u
                act.wait_ge(z2_done, GT * (g + 1))
                if not (isinstance(i, int) and i == 0):
                    act.wait_ge(scattered, 16 * 2 * GT * (g - 1))
                a.activation(rows[:, u].bitcast(F16)[:, :, 0:C], z2[:, u], ACT.Copy).then_inc(zhi, 1)
                act.wait_ge(z2t_psum, g + 1)
                if not (isinstance(i, int) and i == 0):
                    act.wait_ge(logit_psum, g - 1)
                a.activation(zT[:, u], ps[:, 0:CC], ACT.Copy).then_inc(z2t_sb, 1)

            def gap(i, u):
                act.wait_ge(gate_steps, GS * (2 * i + u) + GAP_AT)
                a.activation(wts[:, 1], wts[:, 0], ACT.Exp, scale=1.0 / ZSCALE).then_inc(gap_exp, 1)

            staged(act, NG, [(z2_side, 0), (gap, 1), (lambda i, u: high_half(i + NG // 2, NG + 2 * i + u, u), 0)])

            def hi_part(i, u):
                j = 2 * i + u
                for k in range(4):
                    act.wait_ge(hx_done, 4 * j + k + 1)
                    if k == 0 and not (isinstance(i, int) and i == 0):
                        act.wait_ge(l2_psum, j - 1)
                    a.activation(hhi[:, u, 2 * k:2 * k + 2].rearrange("p h n -> p (h n)"), hx[:, k],
                                 ACT.Relu).then_inc(hi_done, 1)

            def zin_copy(i, u):
                j = 2 * i + u
                act.wait_ge(zin_psum, j + 1)
                if not (isinstance(i, int) and i == 0):
                    act.wait_ge(l1_psum, 4 * (j - 1))
                a.activation(zin[:, u].rearrange("p c n -> p (c n)"), ps[:, 6 + u].bitcast(F16),
                             ACT.Copy).then_inc(zin_sb, 1)

            def meta_copy(i, u):
                j = 2 * i + u
                act.wait_ge(rows_in[u], 16 * (i + 1))
                if not (isinstance(i, int) and i == 0):
                    act.wait_ge(added, 32 * (j - 1))
                a.activation(meta[:, u, :, E:E + 1], rin[:, u, :, TOK:TOK + 1], ACT.Copy).then_inc(meta_done, 1)
                a.activation(meta[:, u, :, 0:E].bitcast(F32), rin[:, u, :, COMB:COMB + E].bitcast(F32),
                             ACT.Copy).then_inc(meta_done, 1)

            def weigh(i, u):
                j = 2 * i + u
                e = act.value_load(tile_exp[0:1, dyn(j)], min_val=0, max_val=E - 1)
                act.wait_ge(meta_done, 2 * (j + 1))
                for h in range(2):
                    act.wait_ge(yv_done, 2 * j + h + 1)
                    a.activation(y[:, u, h], yv[:, h], ACT.Copy,
                                 scale=meta[:, u, h].bitcast(F32)[:, dyn(e)]).then_inc(y_done, 1)

            act.wait_ge(tables, 1)
            staged(act, NT, [(meta_copy, 2), (hi_part, 1), (zin_copy, 0), (weigh, 2)])

        @block.vector
        def _(dve):
            v = nc.vector

            def power(dst, src, tmp, up, step):
                step(v.tensor_scalar(tmp.bitcast(I32), src.bitcast(I32), 23, 23, ALU.logical_shift_right,
                                     ALU.logical_shift_left))
                step(v.tensor_scalar(up, tmp, 1.0 / TOP, None, ALU.mult))
                step(v.reciprocal(dst, up))

            def chain(semaphore, base):
                count = [0]

                def step(ins):
                    ins.then_inc(semaphore, 1)
                    count[0] += 1
                    dve.wait_ge(semaphore, base + count[0])
                return step, count

            v.memset(pad[:], 0).then_inc(pad_out, 1)
            v.memset(kv_bd[:], 0.0).then_inc(kv_ones, 1)
            v.memset(kv[:], 1.0).then_inc(kv_ones, 1)
            dve.wait_ge(pad_out, 2)
            v.memset(pad[:, :, TOK:TOK + 1], T).then_inc(pad_out, 1)
            dve.wait_ge(consts, NCONST)
            dve.wait_ge(kv_ones, 2)

            def w_abs(n, kind, i):
                dve.wait_ge(w_in[kind], 16 * (i + 1))
                if not (isinstance(n, int) and n < 2):
                    dve.wait_ge(wabs_all, n - 1)
                v.tensor_reduce(am[:, kind:kind + 1], stage[:, kind], AX.X, ALU.max,
                                apply_absolute_value=True).then_inc(wabs, 1)

            def w_scale(n, e, kind):
                dve.wait_ge(wabs_all, n + 1)
                step, count = chain(wscale_s, 4 * n)
                if not (isinstance(n, int) and n < 2):
                    dve.wait_ge(whi, 2 * (n - 1))
                top = wmax[:, dyn(e), kind]
                step(v.tensor_scalar(top, amr[:, kind:kind + 1], TINY, None, ALU.max))
                step(v.tensor_scalar(wt[:, kind:kind + 1].bitcast(I32), top.bitcast(I32), 23, 23,
                                     ALU.logical_shift_right, ALU.logical_shift_left))
                step(v.tensor_scalar(winv[:, dyn(e), kind], wt[:, kind:kind + 1], 1.0 / TOP, None, ALU.mult))
                step(v.tensor_scalar(am[:, kind:kind + 1], wt[:, kind:kind + 1], 1.0 / TOP, None, ALU.mult))
                v.reciprocal(wsc[:, kind:kind + 1], am[:, kind:kind + 1]).then_inc(wscale, 1)

            def layernorm(src, dst, n, stats, aggr, rs, zdone, scale):
                for j in range(GT):
                    v.bn_stats(st[:, j], src[:, j]).then_inc(stats, 1)
                dve.wait_ge(stats, GT * (n + 1))
                dve.sem_inc(dve_go, 1)
                for j in range(GT):
                    v.bn_aggr(mv[:, j], st[:, j]).then_inc(aggr, 1)
                dve.wait_ge(aggr, GT * (n + 1))
                step, count = chain(rs, RSTEPS * n)
                step(v.tensor_scalar(ve[:], mv[:, :, 1], LN_EPS, 1.0 / scale ** 2, ALU.add, ALU.mult))
                step(v.tensor_scalar(half[:], ve[:].bitcast(I32), 1, None, ALU.logical_shift_right))
                step(v.tensor_scalar(rstd[:].bitcast(I32), half[:], -1.0, float(0x5F3759DF), ALU.mult, ALU.add))
                for _ in range(3):
                    step(v.tensor_tensor(nt[:, 0], rstd[:], ve[:], ALU.mult))
                    step(v.scalar_tensor_tensor(nt[:, 1], nt[:, 0], -0.5, rstd[:], ALU.mult, ALU.mult))
                    step(v.scalar_tensor_tensor(rstd[:], nt[:, 1], 1.5, rstd[:], ALU.add, ALU.mult))
                assert count[0] == RSTEPS
                for j in range(GT):
                    v.tensor_scalar(dst[:, j], src[:, j], mv[:, j, 0:1], rstd[:, j:j + 1],
                                    ALU.subtract, ALU.mult).then_inc(zdone, 1)

            def norm1(i, u):
                g = 2 * i + u
                dve.wait_ge(x_in[u], 16 * (i + 1))
                if not (isinstance(g, int) and g == 0):
                    dve.wait_ge(zt_psum, g)
                    dve.wait_ge(z1, GT * g)
                layernorm(xr[:, u], z, g, stats1, aggr1, rstd1, z1, 1.0)

            def kq(i, u):
                g = 2 * i + u

                def bias(j):
                    n = GT * g + j
                    dve.wait_ge(kv_psum, n + 1)
                    if not (isinstance(g, int) and g == 0):
                        dve.wait_ge(kv_sum, n - GT + 1)
                    v.tensor_tensor(kv[:, j, :, 0:D], ps[:, 4 + j % 2].rearrange("p (h d) -> p h d", d=D),
                                    bkv_sb[:], ALU.add).then_inc(kv_biased, 1)

                def k_fin(j):
                    dve.wait_ge(k_act, 2 * (GT * g + j + 1))
                    v.scalar_tensor_tensor(kf[:, j], kexp[:, j % 2], 1.0, kf[:, j],
                                           ALU.min, ALU.add).then_inc(k_done, 1)

                bias(0)
                bias(1)
                k_fin(0)
                bias(2)
                k_fin(1)
                bias(3)
                k_fin(2)
                k_fin(3)
                for f in range(CC):
                    dve.wait_ge(q_act, 2 * (CC * g + f + 1))
                    v.scalar_tensor_tensor(qt[:, u, f], qt[:, u, f], 1.0, qrelu[:],
                                           ALU.min, ALU.add).then_inc(q_done, 1)

            dve.wait_ge(params_in, 16 * NPARAM)
            v.tensor_copy(ident16[:], ident[:])
            v.tensor_copy(rev[:], rev_i[:])
            v.tensor_copy(base[:], base_i[:])
            v.tensor_copy(start_row[:], base_i[:])
            v.tensor_copy(tile_no[:], tiles_i[:])
            v.tensor_scalar(low[:], low_i[:], 0, None, ALU.is_ge)
            v.tensor_reduce(b1max[:], b1_sb[:], AX.X, ALU.max, apply_absolute_value=True).then_inc(h_steps, 1)

            staged(dve, NG, [(norm1, 0), (lambda i, u: w_abs(2 * i + u, u, i), 0), (kq, 1),
                             (lambda i, u: w_scale(2 * i + u, i, u), 0)])

            dve.wait_ge(kv_sum, GT * NG)
            for f in range(CC):
                for h in range(HB):
                    v.tensor_copy(kv_bd[h * D:(h + 1) * D, f, h * VW:(h + 1) * VW],
                                  ps[h * D:(h + 1) * D, 2 + f, h * VW:(h + 1) * VW]).then_inc(kvbd, 1)

            v.memset(msum[:].bitcast(I32), 0).then_inc(kv_ones, 1)
            v.memset(rows[:], 0).then_inc(kv_ones, 1)
            dve.wait_ge(kv_ones, 4)

            def attend(i, u):
                g = 2 * i + u
                o = x2[:]
                if not (isinstance(g, int) and g == 0):
                    dve.wait_ge(x2_out, 16 * g)
                    dve.wait_ge(att, GT * g)
                dve.wait_ge(num_psum, GT * (g + 1))
                nd = ps[:, 4:4 + GT, 0:NH * VW].rearrange("p j (h w) -> p j h w", w=VW)
                v.tensor_scalar(den[:], nd[:, :, :, D], ATT_EPS, None, ALU.add).then_inc(dens, 1)
                dve.wait_ge(dens, g + 1)
                v.reciprocal(rden[:], den[:]).then_inc(rdens, 1)
                dve.wait_ge(rdens, g + 1)
                for j in range(GT):
                    v.tensor_tensor(o[:, j].rearrange("p (h d) -> p h d", d=D), nd[:, j, :, 0:D],
                                    rden[:, j].unsqueeze(2).broadcast_to([P, NH, D]), ALU.mult).then_inc(att, 1)
                dve.wait_ge(att, GT * (g + 1))
                dve.wait_ge(x_in[u], 16 * (NG // 2 + i + 1))
                v.tensor_tensor(o, o, xr[:, u], ALU.add).then_inc(x2_done, 1)
                dve.wait_ge(x2_done, g + 1)
                if not (isinstance(i, int) and i == 0):
                    dve.wait_ge(row_data, 3 * (g - 1))
                    dve.wait_ge(z2t_psum, g - 1)
                if not (isinstance(g, int) and g == 0):
                    dve.wait_ge(z2_done, GT * g)
                layernorm(o, z2[:, u], g, stats2, aggr2, rstd2, z2_done, ZSCALE)

            def gate(i, u):
                g = 2 * i + u
                ri = rows[:, u]
                rh = rows[:, u].bitcast(F16)
                rf = rows[:, u].bitcast(F32)
                dve.wait_ge(zhi, g + 1)
                v.tensor_tensor(rh[:, :, C:2 * C], z2[:, u], rh[:, :, 0:C], ALU.subtract).then_inc(row_data, 1)
                v.tensor_copy(ri[:, :, TOK], tok_ids[:, dyn(g)].rearrange("p a j -> p (a j)")).then_inc(row_data, 1)
                dve.wait_ge(logit_psum, g + 1)
                step, count = chain(gate_steps, GS * g)

                def wide(ap):
                    return ap.unsqueeze(2).broadcast_to([P, GT, E])

                def pick(logits, k, mask):
                    step(v.tensor_reduce(mx[:, k], logits[:], AX.X, ALU.max))
                    step(v.tensor_tensor(eq[:], logits[:], wide(mx[:, k]), ALU.is_equal))
                    step(v.tensor_tensor(cand[:], eq[:], rev[:], ALU.mult))
                    step(v.tensor_reduce(first[:], cand[:], AX.X, ALU.max))
                    step(v.tensor_tensor(mask[:], cand[:], wide(first[:]), ALU.is_equal))

                step(v.tensor_copy(lg[:], ps[:, 2, 0:GT * E].rearrange("p (j e) -> p j e", e=E)))
                pick(lg, 0, m1)
                step(v.scalar_tensor_tensor(lg2[:], m1[:], -3.0e38, lg[:], ALU.mult, ALU.add))
                step(v.tensor_reduce(mx[:, 1], lg2[:], AX.X, ALU.max))
                step(v.tensor_tensor(eq[:], lg2[:], wide(mx[:, 1]), ALU.is_equal))
                step(v.tensor_tensor(cand[:], eq[:], rev[:], ALU.mult))
                step(v.tensor_reduce(first[:], cand[:], AX.X, ALU.max))
                step(v.tensor_tensor(wts[:, 0], mx[:, 1], mx[:, 0], ALU.subtract))
                assert count[0] == GAP_AT
                step(v.tensor_tensor(m2[:], cand[:], wide(first[:]), ALU.is_equal))
                step(v.tensor_tensor(msum[:, 0:GT], m1[:], m2[:], ALU.add))
                dve.wait_ge(gap_exp, g + 1)
                step(v.tensor_scalar(wts[:, 2], wts[:, 1], 1.0, None, ALU.add))
                step(v.reciprocal(wts[:, 3], wts[:, 2]))
                step(v.tensor_tensor(wts[:, 4], wts[:, 1], wts[:, 3], ALU.mult))
                step(v.tensor_tensor(cb[:, 0], m1[:], wide(wts[:, 3]), ALU.mult))
                step(v.tensor_tensor(cb[:, 1], m2[:], wide(wts[:, 4]), ALU.mult))
                v.tensor_tensor(rf[:, :, COMB:COMB + E], cb[:, 0], cb[:, 1], ALU.add).then_inc(row_data, 1)
                dve.wait_ge(rank_psum, g + 1)
                ranks = ps[:, 3, 0:(GT + 1) * E].rearrange("p (j e) -> p j e", e=E)
                step(v.tensor_tensor(pos[:], ranks[:, 0:GT], base[:].unsqueeze(1).broadcast_to([P, GT, E]), ALU.add))
                step(v.tensor_tensor(base[:], base[:], ranks[:, GT], ALU.add))
                assert count[0] == GS
                if not (isinstance(i, int) and i == 0):
                    dve.wait_ge(scattered, 16 * 2 * GT * (g - 1))
                v.tensor_tensor(pos1[:], m1[:], pos[:], ALU.mult).then_inc(pl_steps, 1)
                v.tensor_tensor(eq[:], m2[:], pos[:], ALU.mult).then_inc(pl_steps, 1)
                dve.wait_ge(pl_steps, 3 * g + 2)
                v.tensor_reduce(idx[:, u, 0], pos1[:], AX.X, ALU.add).then_inc(pl_steps, 1)
                dve.wait_ge(pl_steps, 3 * g + 3)
                v.tensor_reduce(idx[:, u, 1], eq[:], AX.X, ALU.add).then_inc(placed, 1)
                dve.wait_ge(placed, g + 1)

            staged(dve, NG, [(attend, 0), (lambda i, u: w_abs(NG + 2 * i + u, u, NG // 2 + i), 0), (gate, 1),
                             (lambda i, u: w_scale(NG + 2 * i + u, NG // 2 + i, u), 0)])

            step, count = chain(tab_steps, 0)
            step(v.tensor_copy(pad_row[:], base[0:1]))
            step(v.tensor_tensor(ends[:], base[0:1], start_row[0:1], ALU.subtract))
            step(v.tensor_scalar(cnt_i[:, 0], ends[:], float(TS - 1), None, ALU.add))
            step(v.tensor_scalar(cnt_i[:, 1], cnt_i[:, 0], TS.bit_length() - 1, None, ALU.logical_shift_right))
            step(v.tensor_copy(ntile[:], cnt_i[:, 1]))
            step(v.tensor_tensor(ends3[:], low[:], ntile[:].unsqueeze(1).broadcast_to([1, E, E]), ALU.mult))
            step(v.tensor_reduce(ends[:], ends3[:], AX.X, ALU.add))
            step(v.tensor_tensor(past[:], tile_no[:].unsqueeze(2).broadcast_to([1, NT, E]),
                                 ends[:].unsqueeze(1).broadcast_to([1, NT, E]), ALU.is_ge))
            step(v.tensor_reduce(tab_f[:, 0], past[:], AX.X, ALU.add))
            step(v.tensor_tensor(past_n[:], past[:], ntile[:].unsqueeze(1).broadcast_to([1, NT, E]), ALU.mult))
            step(v.tensor_reduce(tab_f[:, 1], past_n[:], AX.X, ALU.add))
            step(v.tensor_tensor(tab_f[:, 2], tile_no[:], tab_f[:, 1], ALU.subtract))
            step(v.tensor_scalar(tab_f[:, 3], tab_f[:, 0], float(CAP), None, ALU.mult))
            step(v.scalar_tensor_tensor(tile_row[:], tab_f[:, 2], float(TS), tab_f[:, 3], ALU.mult, ALU.add))
            step(v.tensor_scalar(tile_exp[:], tab_f[:, 0], float(E - 1), None, ALU.min))

            dve.wait_ge(b1_all, 1)
            step(v.scalar_tensor_tensor(htmp[:, 0], wmax[:, :, 0], float(C) ** 0.5 * ZBOUND, b1maxr[:], ALU.mult, ALU.add))
            step(v.tensor_scalar(htmp[:, 1].bitcast(I32), htmp[:, 0].bitcast(I32), 23, 23,
                                 ALU.logical_shift_right, ALU.logical_shift_left))
            step(v.tensor_scalar(hinv[:], htmp[:, 1], 1.0 / TOP, None, ALU.mult))
            step(v.reciprocal(hscale[:], hinv[:]))
            step(v.scalar_tensor_tensor(l1_scale[:], hscale[:], 1.0 / ZSCALE, winv[:, :, 0], ALU.mult, ALU.mult))
            step(v.tensor_tensor(y_scale[:], hinv[:], winv[:, :, 1], ALU.mult))
            step(v.tensor_tensor(b1s[:], b1_sb[:], hscale[:].unsqueeze(2).broadcast_to([P, E, HC]), ALU.mult))
            v.memset(htmp[:], 0.0).then_inc(tables, 1)

            def y_part(i, u, h, e):
                j = 2 * i + u
                if h == 0:
                    dve.wait_ge(l2_psum, j + 1)
                if not (isinstance(j, int) and j == 0):
                    dve.wait_ge(y_done, 2 * (j - 1) + h + 1)
                v.scalar_tensor_tensor(yu[:, h], ps[:, 4 + h, 0:C], y_scale[:, dyn(e)],
                                       b2_sb[:, dyn(e)].rearrange("p a c -> p (a c)"), ALU.mult, ALU.add).then_inc(yu_done, 1)
                dve.wait_ge(yu_done, 2 * j + h + 1)
                v.scalar_tensor_tensor(yv[:, h], ps[:, 4 + h, C:2 * C], y_scale[:, dyn(e)], yu[:, h],
                                       ALU.mult, ALU.add).then_inc(yv_done, 1)

            def hidden(i, u):
                j = 2 * i + u
                e = dve.value_load(tile_exp[0:1, dyn(j)], min_val=0, max_val=E - 1)

                def scaled(k):
                    dve.wait_ge(l1_psum, 4 * j + k + 1)
                    if not (isinstance(j, int) and j == 0):
                        dve.wait_ge(lo_done, 4 * (j - 1) + k + 1)
                    v.scalar_tensor_tensor(
                        hx[:, k].rearrange("p (h n) -> p h n", h=2), ps[:, k].rearrange("p (h n) -> p h n", h=2),
                        l1_scale[:, dyn(e)],
                        b1s[:, dyn(e), 2 * k:2 * k + 2].rearrange("p a h -> p (a h)").unsqueeze(2).broadcast_to([P, 2, TS]),
                        ALU.mult, ALU.add).then_inc(hx_done, 1)

                def lo_part(k):
                    dve.wait_ge(hi_done, 4 * j + k + 1)
                    v.scalar_tensor_tensor(
                        hlo[:, u, 2 * k:2 * k + 2].rearrange("p h n -> p (h n)"), hx[:, k], 0.0,
                        hhi[:, u, 2 * k:2 * k + 2].rearrange("p h n -> p (h n)"), ALU.max, ALU.subtract).then_inc(lo_done, 1)

                if not (isinstance(i, int) and i == 0):
                    dve.wait_ge(l2_psum, j - 1)
                scaled(0)
                scaled(1)
                lo_part(0)
                scaled(2)
                lo_part(1)
                scaled(3)
                lo_part(2)
                lo_part(3)

            def result(i, u):
                e = dve.value_load(tile_exp[0:1, dyn(2 * i + u)], min_val=0, max_val=E - 1)
                y_part(i, u, 0, e)
                y_part(i, u, 1, e)

            dve.wait_ge(tables, 1)
            dve.wait_ge(b2_in, 16)
            staged(dve, NT, [(hidden, 1), (result, 2)])

        @block.tensor
        def _(pe):
            t = nc.tensor
            pe.wait_ge(consts, NCONST)
            pe.wait_ge(params_in, 16 * NPARAM)

            def turn(src, i, u, ready, psum_read, done):
                g = 2 * i + u
                pe.wait_ge(ready, GT * (g + 1))
                if not (isinstance(g, int) and g == 0):
                    pe.wait_ge(psum_read, g)
                for c in range(CC):
                    for j in range(GT):
                        ins = t.transpose(ps[:, c, j * P:(j + 1) * P], src[:, j, c * P:(c + 1) * P], ident[:])
                ins.then_inc(done, 1)

            def project(i, u):
                g = 2 * i + u
                pe.wait_ge(zt_sb, g + 1)
                head = isinstance(g, int) and g == 0
                tail = isinstance(g, int) and g == NG - 1

                def proj(j):
                    n = GT * g + j
                    if not (isinstance(n, int) and n < 2):
                        pe.wait_ge(kv_biased, n - 1)
                    for c in range(CC):
                        ins = t.matmul(ps[:, 4 + j % 2], zT[:, u, c, j * P:(j + 1) * P],
                                       wkv_sb[:, c].rearrange("p k n -> p (k n)"), start=(c == 0), stop=(c == CC - 1))
                    ins.then_inc(kv_psum, 1)

                def add_kv(j):
                    pe.wait_ge(k_done, GT * g + j + 1)
                    for f in range(CC):
                        ins = t.matmul(ps[:, 2 + f, 0:NHC], kf[:, j, f * P:(f + 1) * P],
                                       kv[:, j, NH + f * HB:NH + (f + 1) * HB].rearrange("p h w -> p (h w)"),
                                       start=(head and j == 0), stop=(tail and j == GT - 1))
                    ins.then_inc(kv_sum, 1)

                proj(0)
                proj(1)
                proj(2)
                add_kv(0)
                proj(3)
                add_kv(1)
                for f in range(CC):
                    if not head:
                        pe.wait_ge(q_act, 2 * (CC * (g - 1) + f + 1))
                    for c in range(CC):
                        ins = t.matmul(ps[:, 6 + f], wq_sb[:, c, f * P:(f + 1) * P], zT[:, u, c],
                                       start=(c == 0), stop=(c == CC - 1))
                    ins.then_inc(q_psum, 1)
                add_kv(2)
                add_kv(3)

            staged(pe, NG, [(project, 1), (lambda i, u: turn(z, i, u, z1, zt_sb, zt_psum), 0)])

            pe.wait_ge(kvbd, CC * HB)

            def numerators(i, u):
                g = 2 * i + u
                pe.wait_ge(qt_in[u], 16 * (i + 1))
                for j in range(GT):
                    if not (isinstance(g, int) and g == 0):
                        pe.wait_ge(att, GT * (g - 1) + j + 1)
                    for f in range(CC):
                        ins = t.matmul(ps[:, 4 + j, f * NHC:(f + 1) * NHC], qt[:, u, f, j * P:(j + 1) * P],
                                       kv_bd[:, f], start=True, stop=True)
                    ins.then_inc(num_psum, 1)

            def logits(i, u):
                g = 2 * i + u
                pe.wait_ge(z2t_sb, g + 1)
                if not (isinstance(g, int) and g == 0):
                    pe.wait_ge(gate_steps, GS * (g - 1) + 1)
                for j in range(GT):
                    for c in range(CC):
                        ins = t.matmul(ps[:, 2, j * E:(j + 1) * E], zT[:, u, c, j * P:(j + 1) * P], gw_sb[:, c],
                                       start=(c == 0), stop=(c == CC - 1))
                ins.then_inc(logit_psum, 1)

            def rank(i, u):
                g = 2 * i + u
                pe.wait_ge(gate_steps, GS * g + GAP_AT + 2)
                t.matmul(ps[:, 3, 0:(GT + 1) * E], tri[:], msum[:].rearrange("p j e -> p (j e)"), start=True, stop=False)
                for j in range(GT):
                    ins = t.matmul(ps[:, 3, (j + 1) * E:(GT + 1) * E].rearrange("p (k e) -> p k e", e=E), ones[:],
                                   msum[:, j].unsqueeze(1).broadcast_to([P, GT - j, E]),
                                   start=False, stop=(j == GT - 1))
                ins.then_inc(rank_psum, 1)

            staged(pe, NG, [(numerators, 0), (logits, 1),
                            (lambda i, u: turn(z2[:, u], i, u, z2_done, z2t_sb, z2t_psum), 0), (rank, 1)])

            pe.wait_ge(tables, 1)

            def layer1(i, u):
                j = 2 * i + u
                e = pe.value_load(tile_exp[0:1, dyn(j)], min_val=0, max_val=E - 1)
                pe.wait_ge(zin_sb, j + 1)
                for k in range(4):
                    if not (isinstance(j, int) and j == 0):
                        pe.wait_ge(hx_done, 4 * (j - 1) + k + 1)
                    for h in range(2):
                        col = (2 * k + h) * P
                        n = 0
                        for c in range(CC):
                            whi_ap = w1s[:, dyn(e), 0, c * HC * P + col:c * HC * P + col + P].rearrange("p a n -> p (a n)")
                            wlo_ap = w1s[:, dyn(e), 1, c * HC * P + col:c * HC * P + col + P].rearrange("p a n -> p (a n)")
                            for w, zz in ((whi_ap, c), (whi_ap, CC + c), (wlo_ap, c)):
                                ins = t.matmul(ps[:, k, h * TS:(h + 1) * TS], w, zin[:, u, zz],
                                               start=(n == 0), stop=(n == 3 * CC - 1))
                                n += 1
                    ins.then_inc(l1_psum, 1)

            def layer2(i, u):
                j = 2 * i + u
                e = pe.value_load(tile_exp[0:1, dyn(j)], min_val=0, max_val=E - 1)
                if not (isinstance(j, int) and j == 0):
                    pe.wait_ge(yv_done, 2 * j)
                for c in range(HC):
                    if c % 2 == 0:
                        pe.wait_ge(lo_done, 4 * j + c // 2 + 1)
                    both = w2s[:, dyn(e), c].rearrange("p a k n -> p (a k n)")
                    high = w2s[:, dyn(e), c, 0].rearrange("p a n -> p (a n)")
                    for h in range(2):
                        t.matmul(ps[:, 4 + h], hhi[:, u, c, h * P:(h + 1) * P], both, start=(c == 0), stop=False)
                    for h in range(2):
                        ins = t.matmul(ps[:, 4 + h, C:2 * C], hlo[:, u, c, h * P:(h + 1) * P], high,
                                       start=False, stop=(c == HC - 1))
                ins.then_inc(l2_psum, 1)

            def turn_rows(i, u):
                pe.wait_ge(rows_in[u], 16 * (i + 1))
                if not (isinstance(i, int) and i == 0):
                    pe.wait_ge(zin_sb, 2 * i + u - 1)
                for c in range(2 * CC):
                    for h in range(2):
                        ins = t.transpose(ps[:, 6 + u].bitcast(F16)[:, c * TS + h * P:c * TS + (h + 1) * P],
                                          rin[:, u, h].bitcast(F16)[:, c * P:(c + 1) * P], ident16[:])
                ins.then_inc(zin_psum, 1)

            staged(pe, NT, [(layer1, 1), (turn_rows, 0), (layer2, 2)])


def kernel(**inputs):
    import numpy as _np
    import concourse.bacc as _bacc
    from concourse import mybir as _mybir
    from concourse.bass_utils import run_bass_kernel_spmd as _run

    a = {k: _np.asarray(v) for k, v in inputs.items()}
    B, L, C = a["L0_attn_x"].shape
    E, HID, _ = a["L0_ffn_w1"].shape
    cc, hc = C // 128, HID // 128

    def rows_first(w):
        return w.reshape(cc, 128, -1).transpose(1, 0, 2)

    arrays = {
        "x": a["L0_attn_x"].reshape(B * L, C),
        "wq": rows_first(a["L0_attn_Wq"]), "bq": a["L0_attn_bq"].reshape(cc, 128).T,
        "wk": rows_first(a["L0_attn_Wk"]), "bk": a["L0_attn_bk"],
        "wv": rows_first(a["L0_attn_Wv"]), "bv": a["L0_attn_bv"],
        "gate_w": rows_first(a["L0_ffn_gate_w"].T),
        "w1": a["L0_ffn_w1"].reshape(E, HID, cc, 128).transpose(0, 3, 2, 1).reshape(E, 128, cc * HID),
        "b1": a["L0_ffn_b1"].reshape(E, hc, 128).transpose(2, 0, 1),
        "w2": a["L0_ffn_w2"].reshape(E, C, hc, 128).transpose(0, 3, 2, 1).reshape(E, 128, hc * C),
        "b2": a["L0_ffn_b2"].reshape(E * C),
    }
    arrays = {k: _np.ascontiguousarray(v) for k, v in arrays.items()}
    nc = _bacc.Bacc("TRN2", target_bir_lowering=False, num_devices=1)
    args = [nc.dram_tensor(k, v.shape, _mybir.dt.from_np(v.dtype), kind="ExternalInput").ap()
            for k, v in arrays.items()]
    out = nc.dram_tensor("out", (B * L, C), _mybir.dt.float32, kind="ExternalOutput").ap()
    attention_moe(nc, *args, out)
    r = _run(nc, [arrays], core_ids=[0])
    return r.results[0]["out"].reshape(B, L, C)
```

```python
from contextlib import ExitStack

import concourse.bass as bass
from concourse import mybir

ALU = mybir.AluOpType
ACT = mybir.ActivationFunctionType
AX = mybir.AxisListType
F32 = mybir.dt.float32
F16 = mybir.dt.float16
I32 = mybir.dt.int32
RMAX = bass.bass_isa.ReduceOp.max

P = 128
GT = 4
LN_EPS = 1e-5
ATT_EPS = 1e-6
ZBOUND = 16.0
ZSCALE = 1024.0
TOP = 2.0 ** 14
TINY = 1e-12


def dyn(i, n=1):
    return bass.DynSlice(i, n)


def early(number, count):
    return isinstance(number, int) and number < count


def staged(eng, n, steps, turn=2):
    lags = max(lag for _, lag in steps)

    def slot(i, u, number=None):
        for f, lag in steps:
            if number is None or lag <= number < n + lag:
                back = -((u - lag) // turn)
                f(i - back if back else i, (u - lag) % turn)
    for k in range(4):
        slot(k // turn, k % turn, k)
    with eng.Fori(4 // turn, n // turn) as i:
        for u in range(turn):
            slot(i, u)
    for k in range(n // turn * turn, n + lags):
        slot(k // turn, k % turn, k)


def attention_moe(nc, x, wq, bq, wk, bk, wv, bv, gate_w, w1, b1, w2, b2, out):
    T, C = x.shape
    E = gate_w.shape[2]
    HC = b1.shape[2]
    CC = C // P
    NH = 8
    D = C // NH
    HB = P // D
    NG = T // (GT * P)
    TS = 2 * P
    NT = (2 * T + E * (TS - 1)) // TS
    CAP = T + TS
    SPARE = NT - 2 * T // TS
    ROW = C + 16
    COMB, TOK = C, C + E
    RING = 4
    VW = D + 1
    NHC = HB * VW
    PIECE = HC * C
    assert 2 * E == 2 * NG and NG % 2 == 0

    scratch = nc.dram_tensor("rows_by_expert", [E * CAP + SPARE * TS, ROW], I32, kind="Internal").ap()
    qt_dram = nc.dram_tensor("q_transposed", [NG, P, CC * GT * P], F32, kind="Internal").ap()
    x_v = x.rearrange("(g p j) c -> g p (j c)", p=P, j=GT)
    out_v = out.rearrange("(g p j) c -> g p (j c)", p=P, j=GT)

    with ExitStack() as ctx:
        def sb(name, shape, dt=F32, scope=ctx):
            return scope.enter_context(nc.sbuf_tensor(name, shape, dt))

        def sem(name):
            return ctx.enter_context(nc.semaphore(name))

        ps = ctx.enter_context(nc.psum_tensor("ps", [P, 8, 512], F32))
        w1s = sb("w1_split", [P, E, 2, PIECE], F16)
        w2s = sb("w2_split", [P, E, HC, 2, C], F16)
        ident = sb("ident", [P, P])
        tri = sb("tri", [P, P], F16)
        ones = sb("ones", [P, P], F16)
        ident16 = sb("ident16", [P, P], F16)
        wkv_sb = sb("wkv_sb", [P, CC, 2, C])
        bq_sb = sb("bq_sb", [P, CC])
        gw_sb = sb("gw_sb", [P, CC, E])
        b1_sb = sb("b1_sb", [P, E, HC])
        b1s = sb("b1_scaled", [P, E, HC])
        kv_bd = sb("kv_blockdiag", [P, CC, NHC])
        pad = sb("pad_rows", [P, ROW], I32)
        tok_ids = sb("tok_ids", [P, NG, GT], I32)
        wmax = sb("wmax", [P, E, 2])
        winv = sb("winv", [P, E, 2])
        b1max = sb("b1max", [P, E])
        b1maxr = sb("b1maxr", [P, E])
        hscale = sb("hscale", [P, E])
        hinv = sb("hinv", [P, E])
        htmp = sb("htmp", [P, 2, E])
        l1_scale = sb("l1_scale", [P, E])
        y_scale = sb("y_scale", [P, E])
        am = sb("am", [P, 2])
        amr = sb("amr", [P, 2])
        wt = sb("wt", [P, 2])
        wsc = sb("wsc", [P, 2])
        rev = sb("rev", [P, GT, E])
        base = sb("base", [P, E])
        start_row = sb("start_row", [P, E])
        tile_no = sb("tile_no", [1, NT])
        low = sb("low", [1, E, E])
        cnt_i = sb("cnt_i", [1, 2, E], I32)
        ntile = sb("ntile", [1, E])
        ends = sb("ends", [1, E])
        ends3 = sb("ends3", [1, E, E])
        past = sb("past", [1, NT, E])
        past_n = sb("past_n", [1, NT, E])
        tab_f = sb("tab_f", [1, 4, NT])
        pad_row = sb("pad_row", [1, E], I32)
        tile_row = sb("tile_row", [1, NT], I32)
        tile_exp = sb("tile_exp", [1, NT], I32)

        s12 = ExitStack()
        xr = sb("x_ring", [P, 2, GT, C], scope=s12)
        qt = sb("qt_ring", [P, 2, CC, GT * P], scope=s12)
        stage = sb("w_stage", [P, 2, PIECE], scope=s12)
        st = sb("bn_st", [P, GT, 6], scope=s12)
        mv = sb("mean_var", [P, GT, 2], scope=s12)
        rstd = sb("rstd", [P, GT], scope=s12)
        ve = sb("ve", [P, GT], scope=s12)
        half = sb("half", [P, GT], I32, scope=s12)
        nt = sb("newton", [P, 2, GT], scope=s12)
        zT = sb("zT", [P, 2, CC, GT * P], scope=s12)
        s1 = ExitStack()
        wq_sb = sb("wq_sb", [P, CC, C], scope=s1)
        bkv_sb = sb("bkv_sb", [P, 2 * NH, D], scope=s1)
        z = sb("z", [P, GT, C], scope=s1)
        kv = sb("kv", [P, GT, 2 * NH, VW], scope=s1)
        kf = sb("kf", [P, GT, C], scope=s1)
        s0 = ExitStack()
        rev_i = sb("rev_i", [P, GT, E], I32, scope=s0)
        base_i = sb("base_i", [P, E], I32, scope=s0)
        tiles_i = sb("tiles_i", [1, NT], I32, scope=s0)
        low_i = sb("low_i", [1, E, E], I32, scope=s0)
        s0.close()
        kexp = sb("kexp", [P, 2, C], scope=s1)
        qrelu = sb("qrelu", [P, CC, GT * P], scope=s1)
        s1.close()
        x2 = sb("x2", [P, GT, C], scope=s12)
        z2 = sb("z2", [P, 2, GT, C], scope=s12)
        rows = sb("rows", [P, 2, GT, ROW], I32, scope=s12)
        den = sb("den", [P, GT, NH], scope=s12)
        rden = sb("rden", [P, GT, NH], scope=s12)
        lg = sb("lg", [P, GT, E], scope=s12)
        lg2 = sb("lg2", [P, GT, E], scope=s12)
        eq = sb("eq", [P, GT, E], scope=s12)
        cand = sb("cand", [P, GT, E], scope=s12)
        mx = sb("mx", [P, 2, GT], scope=s12)
        first = sb("first", [P, GT], scope=s12)
        m1 = sb("m1", [P, GT, E], scope=s12)
        m2 = sb("m2", [P, GT, E], scope=s12)
        msum = sb("msum", [P, GT + 1, E], F16, scope=s12)
        wts = sb("wts", [P, 5, GT], scope=s12)
        cb = sb("cb", [P, 2, GT, E], scope=s12)
        pos = sb("pos", [P, GT, E], scope=s12)
        pos1 = sb("pos1", [P, GT, E], scope=s12)
        idx = sb("idx", [P, 2, 2, GT], I32, scope=s12)
        s12.close()
        rin = sb("rin", [P, RING, 2, ROW], I32)
        zin = sb("zin", [P, 2, 2 * CC, TS], F16)
        meta = sb("meta", [P, RING, 2, 16], I32)
        hx = sb("hx", [P, 4, 512])
        hhi = sb("hhi", [P, 2, HC, TS], F16)
        hlo = sb("hlo", [P, 2, HC, TS], F16)
        b2_sb = sb("b2_sb", [P, E, C])
        yu = sb("yu", [P, 2, C])
        yv = sb("yv", [P, 2, C])
        y = sb("y", [P, 2, 2, C])

        names = """consts kv_ones pad_out spare_out b2_in
            stats1 aggr1 rstd1 z1 zt_psum zt_sb q_psum q_act q_done kv_psum kv_biased k_act k_done kv_sum
            kvbd wabs wabs_all wscale_s wscale whi wlo
            num_psum dens rdens att x2_done stats2 aggr2 rstd2 z2_done z2t_psum z2t_sb zhi row_data
            logit_psum gate_steps gap_exp rank_psum placed pl_steps
            h_steps b1_all tab_steps tables pads_out
            l1_psum hx_done hi_done lo_done l2_psum yu_done yv_done y_done added""".split()
        s = {n: sem(n) for n in names}
        (consts, kv_ones, pad_out, spare_out, b2_in,
         stats1, aggr1, rstd1, z1, zt_psum, zt_sb, q_psum, q_act, q_done, kv_psum, kv_biased, k_act,
         k_done, kv_sum, kvbd, wabs, wabs_all, wscale_s, wscale, whi, wlo,
         num_psum, dens, rdens, att, x2_done, stats2, aggr2, rstd2, z2_done, z2t_psum, z2t_sb, zhi,
         row_data, logit_psum, gate_steps, gap_exp, rank_psum, placed, pl_steps,
         h_steps, b1_all, tab_steps, tables, pads_out,
         l1_psum, hx_done, hi_done, lo_done, l2_psum, yu_done, yv_done, y_done, added) = (s[n] for n in names)
        params_in = sem("params_in")
        x_in = [sem("x_in0"), sem("x_in1")]
        w_in = [sem("w_in0"), sem("w_in1")]
        qt_out = [sem("qt_out0"), sem("qt_out1")]
        qt_in = [sem("qt_in0"), sem("qt_in1")]
        x2_out = sem("x2_out")
        scattered = [sem("scattered0"), sem("scattered1")]
        rows_in = [sem(f"rows_in{u}") for u in range(RING)]
        zin_psum, zin_sb, meta_done = sem("zin_psum"), sem("zin_sb"), sem("meta_done")
        NPARAM = 8
        NCONST = 9
        pool_go, dve_go = sem("pool_go"), sem("dve_go")

        RSTEPS = 12
        GS, GAP_AT = 21, 12
        ctx.enter_context(nc.allow_low_precision(reason="row numbers, summed in float32 into int32, are exact"))
        block = ctx.enter_context(nc.Block())

        @block.sync
        def _(sp):
            def load_w(i, kind):
                src = (w1 if kind == 0 else w2)[dyn(i)].rearrange("a p n -> p (a n)")
                sp.dma_start(stage[:, kind], src).then_inc(w_in[kind], 16)

            sp.dma_start(xr[:, 0].rearrange("p j c -> p (j c)"), x_v[0]).then_inc(x_in[0], 16)
            sp.dma_start(wkv_sb[:, :, 0], wk).then_inc(params_in, 16)
            sp.dma_start(wkv_sb[:, :, 1], wv).then_inc(params_in, 16)
            sp.dma_start(bkv_sb[:, 0:NH].rearrange("p h d -> p (h d)"), bk.partition_broadcast(P)).then_inc(params_in, 16)
            sp.dma_start(bkv_sb[:, NH:].rearrange("p h d -> p (h d)"), bv.partition_broadcast(P)).then_inc(params_in, 16)
            sp.dma_start(wq_sb[:], wq).then_inc(params_in, 16)
            sp.dma_start(bq_sb[:], bq).then_inc(params_in, 16)
            sp.dma_start(gw_sb[:], gate_w).then_inc(params_in, 16)
            sp.dma_start(b1_sb[:], b1).then_inc(params_in, 16)
            load_w(0, 0)
            sp.dma_start(xr[:, 1].rearrange("p j c -> p (j c)"), x_v[1]).then_inc(x_in[1], 16)
            load_w(0, 1)
            sp.wait_ge(pad_out, 3)
            for k in range(SPARE):
                lo = E * CAP + k * TS
                sp.dma_start(scratch[lo:lo + TS].rearrange("(p s) r -> p s r", p=P),
                             pad[:].unsqueeze(1).broadcast_to([P, TS // P, ROW])).then_inc(spare_out, 16)

            def load_x(i, u):
                if not early(i, 1):
                    sp.wait_ge(z1, GT * (2 * i + u - 1))
                    sp.dma_start(xr[:, u].rearrange("p j c -> p (j c)"),
                                 x_v[dyn(2 * i + u)].rearrange("a p n -> p (a n)")).then_inc(x_in[u], 16)

            def store_q(i, u):
                sp.wait_ge(q_done, CC * (2 * i + u + 1))
                sp.dma_start(qt_dram[dyn(2 * i + u)].rearrange("a p n -> p (a n)"),
                             qt[:, u].rearrange("p c n -> p (c n)")).then_inc(qt_out[u], 16)

            def load_w1(i, u):
                if not early(i, 1):
                    sp.wait_ge(wlo, 2 * i + u - 1)
                    load_w(i, u)

            staged(sp, NG, [(load_x, 0), (store_q, 3), (load_w1, 1)])

            H2 = NG // 2

            def load2(i, u):
                g = 2 * i + u
                if early(i, 1):
                    sp.wait_ge(z1, GT * (NG - 1 + u))
                else:
                    sp.wait_ge(x2_done, g - 1)
                sp.dma_start(xr[:, u].rearrange("p j c -> p (j c)"),
                             x_v[dyn(g)].rearrange("a p n -> p (a n)")).then_inc(x_in[u], 16)
                sp.wait_ge(qt_out[u], 16 * H2)
                if not early(i, 1):
                    sp.wait_ge(num_psum, GT * (g - 1))
                sp.dma_start(qt[:, u].rearrange("p c n -> p (c n)"),
                             qt_dram[dyn(g)].rearrange("a p n -> p (a n)")).then_inc(qt_in[u], 16)

            def load_w2(i, u):
                sp.wait_ge(wlo, NG + 2 * i + u - 1)
                load_w(i + H2, u)

            def store_x2(i, u):
                sp.wait_ge(x2_done, 2 * i + u + 1)
                sp.dma_start(out_v[dyn(2 * i + u)].rearrange("a p n -> p (a n)"),
                             x2[:].rearrange("p j c -> p (j c)")).then_inc(x2_out, 16)

            staged(sp, NG, [(load2, 0), (store_x2, 2), (load_w2, 1)])

            sp.wait_ge(tables, 1)
            for e in range(E):
                r = sp.value_load(pad_row[0:1, e:e + 1], min_val=0, max_val=E * CAP - TS)
                sp.dma_start(scratch[dyn(r, TS)].rearrange("(p s) r -> p s r", p=P),
                             pad[:].unsqueeze(1).broadcast_to([P, TS // P, ROW])).then_inc(pads_out, 16)
            sp.wait_ge(spare_out, 16 * SPARE)
            sp.wait_ge(pads_out, 16 * E)
            for u in range(2):
                sp.wait_ge(scattered[u], 16 * GT * NG)

            def load_rows(i, u):
                j = RING * i + u
                if early(i, 1) and u == 2:
                    sp.wait_ge(wlo, 2 * NG)
                    sp.wait_ge(x2_out, 16 * NG)
                    sp.dma_start(b2_sb[:].rearrange("p e c -> p (e c)"), b2.partition_broadcast(P)).then_inc(b2_in, 16)
                r = sp.value_load(tile_row[0:1, dyn(j)], min_val=0, max_val=E * CAP + (SPARE - 1) * TS)
                if not early(i, 1):
                    sp.wait_ge(meta_done, 2 * (j - RING + 1))
                sp.dma_start(rin[:, u].rearrange("p h r -> p (h r)"),
                             scratch[dyn(r, TS)].rearrange("(p h) r -> p (h r)", p=P)).then_inc(rows_in[u], 16)

            staged(sp, NT, [(load_rows, 0)], turn=RING)

        @block.gpsimd
        def _(pool):
            g = nc.gpsimd
            g.memset(ident[:], 0.0).then_inc(consts, 1)
            g.memset(tri[:], 1.0).then_inc(consts, 1)
            g.memset(ones[:], 1.0).then_inc(consts, 1)
            pool.wait_ge(consts, 3)
            g.affine_select(out=ident[:], in_=ident[:], compare_op=ALU.not_equal, fill=1.0, base=0,
                            pattern=[[-1, P]], channel_multiplier=1).then_inc(consts, 1)
            g.affine_select(out=tri[:], in_=tri[:], compare_op=ALU.is_gt, fill=0.0, base=0,
                            pattern=[[1, P]], channel_multiplier=-1).then_inc(consts, 1)
            g.iota(rev_i[:], pattern=[[0, GT], [-1, E]], base=E, channel_multiplier=0).then_inc(consts, 1)
            g.iota(base_i[:], pattern=[[CAP, E]], base=0, channel_multiplier=0).then_inc(consts, 1)
            g.iota(tiles_i[:], pattern=[[1, NT]], base=0, channel_multiplier=0).then_inc(consts, 1)
            g.iota(low_i[:], pattern=[[1, E], [-1, E]], base=0, channel_multiplier=0).then_inc(consts, 1)
            g.iota(tok_ids[:], pattern=[[GT * P, NG], [1, GT]], base=0, channel_multiplier=GT).then_inc(pad_out, 1)

            def all_max(n, u):
                pool.wait_ge(wabs, n + 1)
                if not early(n, 2):
                    pool.wait_ge(wscale, n - 1)
                pool.sem_inc(pool_go, 1)
                g.partition_all_reduce(amr[:, u:u + 1], am[:, u:u + 1], P, RMAX).then_inc(wabs_all, 1)

            def low_half(e, n, kind):
                pool.wait_ge(whi, 2 * (n + 1))
                if kind == 0:
                    hi, lo = w1s[:, dyn(e), 0].rearrange("p a n -> p (a n)"), w1s[:, dyn(e), 1].rearrange("p a n -> p (a n)")
                    g.tensor_tensor(lo, stage[:, 0], hi, ALU.subtract).then_inc(wlo, 1)
                else:
                    hi = w2s[:, dyn(e), :, 0].rearrange("p a h c -> p (a h) c")
                    lo = w2s[:, dyn(e), :, 1].rearrange("p a h c -> p (a h) c")
                    g.tensor_tensor(lo, stage[:, 1].rearrange("p (h c) -> p h c", h=HC), hi,
                                    ALU.subtract).then_inc(wlo, 1)

            staged(pool, NG, [(lambda i, u: all_max(2 * i + u, u), 0), (lambda i, u: low_half(i, 2 * i + u, u), 1)])
            pool.wait_ge(h_steps, 1)
            g.partition_all_reduce(b1maxr[:], b1max[:], P, RMAX).then_inc(b1_all, 1)

            def scatter(i, u):
                n = 2 * i + u
                pool.wait_ge(placed, n + 1)
                pool.wait_ge(row_data, 3 * (n + 1))
                pool.sem_inc(pool_go, 1)
                for j in range(GT):
                    for k in range(2):
                        g.indirect_dma_start(
                            out=scratch, out_offset=bass.IndirectOffsetOnAxis(ap=idx[:, u, k, j:j + 1], axis=0),
                            in_=rows[:, u, j], in_offset=None).then_inc(scattered[u], 16)

            def low_and_scatter(i, u):
                last = isinstance(i, int) and 2 * i + u == NG - 1
                if last:
                    scatter(i, u)
                low_half(i + NG // 2, NG + 2 * i + u, u)
                if not last:
                    scatter(i, u)

            staged(pool, NG, [(lambda i, u: all_max(NG + 2 * i + u, u), 0), (low_and_scatter, 1)])

            pool.wait_ge(x2_out, 16 * NG)

            def add_rows(i, u):
                n = RING * i + u
                for h in range(2):
                    pool.wait_ge(y_done, 2 * n + h + 1)
                    if not early(2 * n + h, 1):
                        pool.wait_ge(added, 16 * (2 * n + h))
                    pool.sem_inc(pool_go, 1)
                    g.indirect_dma_start(
                        out=out, out_offset=bass.IndirectOffsetOnAxis(ap=meta[:, u, h, E:E + 1], axis=0),
                        in_=y[:, u % 2, h], in_offset=None, bounds_check=T - 1, oob_is_err=False,
                        compute_op=ALU.add).then_inc(added, 16)

            staged(pool, NT, [(add_rows, 0)], turn=RING)
            pool.wait_ge(added, 32 * NT)

        @block.scalar
        def _(act):
            a = nc.scalar

            def scale_piece(e, n, kind):
                act.wait_ge(wscale, n + 1)
                a.activation(stage[:, kind], stage[:, kind], ACT.Copy, scale=wsc[:, kind:kind + 1]).then_inc(whi, 1)

            def round_piece(e, n, kind):
                act.wait_ge(whi, 2 * n + 1)
                if kind == 0:
                    a.activation(w1s[:, dyn(e), 0].rearrange("p a n -> p (a n)"), stage[:, 0], ACT.Copy).then_inc(whi, 1)
                else:
                    a.activation(w2s[:, dyn(e), :, 0].rearrange("p a h c -> p (a h) c"),
                                 stage[:, 1].rearrange("p (h c) -> p h c", h=HC), ACT.Copy).then_inc(whi, 1)

            def zt_copy(i, u):
                g = 2 * i + u
                act.wait_ge(zt_psum, g + 1)
                if not early(i, 1):
                    act.wait_ge(kv_sum, GT * (g - 1))
                a.activation(zT[:, u], ps[:, 0:CC], ACT.Copy).then_inc(zt_sb, 1)

            def k_tile(i, u, j):
                n = GT * (2 * i + u) + j
                act.wait_ge(kv_biased, n + 1)
                if not early(n, 2):
                    act.wait_ge(k_done, n - 1)
                kin = kv[:, j, 0:NH, 0:D]
                a.activation(kexp[:, j % 2].rearrange("p (h d) -> p h d", h=NH), kin, ACT.Exp).then_inc(k_act, 1)
                if not early(n, GT):
                    act.wait_ge(kv_sum, n - GT + 1)
                a.activation(kf[:, j].rearrange("p (h d) -> p h d", h=NH), kin, ACT.Relu).then_inc(k_act, 1)

            def q_chunk(i, u, f):
                g = 2 * i + u
                if f == 0 and not early(i, 1):
                    act.wait_ge(qt_out[u], 16 * i)
                act.wait_ge(q_psum, CC * g + f + 1)
                a.activation(qt[:, u, f], ps[:, 6 + f], ACT.Exp, bias=bq_sb[:, f:f + 1]).then_inc(q_act, 1)
                if not early(g, 1):
                    act.wait_ge(q_done, CC * (g - 1) + f + 1)
                a.activation(qrelu[:, f], ps[:, 6 + f], ACT.Relu, bias=bq_sb[:, f:f + 1]).then_inc(q_act, 1)

            def first_side(i, u):
                for j in range(GT - 1):
                    k_tile(i, u, j)
                scale_piece(i, 2 * i + u, u)
                k_tile(i, u, GT - 1)
                q_chunk(i, u, 0)

            def second_side(i, u):
                round_piece(i, 2 * i + u, u)
                q_chunk(i, u, 1)

            act.wait_ge(params_in, 16 * NPARAM)
            staged(act, NG, [(first_side, 1), (zt_copy, 0), (second_side, 1)])

            def z2_side(i, u):
                g = 2 * i + u
                act.wait_ge(z2_done, GT * (g + 1))
                if not early(i, 1):
                    act.wait_ge(scattered[u], 16 * 2 * GT * i)
                a.activation(rows[:, u].bitcast(F16)[:, :, 0:C], z2[:, u], ACT.Copy).then_inc(zhi, 1)
                act.wait_ge(z2t_psum, g + 1)
                if not early(i, 1):
                    act.wait_ge(logit_psum, g - 1)
                a.activation(zT[:, u], ps[:, 0:CC], ACT.Copy).then_inc(z2t_sb, 1)

            def gap(i, u):
                act.wait_ge(gate_steps, GS * (2 * i + u) + GAP_AT)
                a.activation(wts[:, 1], wts[:, 0], ACT.Exp, scale=1.0 / ZSCALE).then_inc(gap_exp, 1)

            staged(act, NG, [(z2_side, 0), (lambda i, u: scale_piece(i + NG // 2, NG + 2 * i + u, u), 0),
                             (gap, 0), (lambda i, u: round_piece(i + NG // 2, NG + 2 * i + u, u), 0)])

            def hi_part(i, u):
                j = RING * i + u
                for k in range(4):
                    act.wait_ge(hx_done, 4 * j + k + 1)
                    if k == 0 and not early(j, 2):
                        act.wait_ge(l2_psum, j - 1)
                    a.activation(hhi[:, u % 2, 2 * k:2 * k + 2].rearrange("p h n -> p (h n)"), hx[:, k],
                                 ACT.Relu).then_inc(hi_done, 1)

            def zin_copy(i, u):
                j = RING * i + u
                act.wait_ge(zin_psum, j + 1)
                if not early(j, 2):
                    act.wait_ge(l1_psum, 4 * (j - 1))
                a.activation(zin[:, u % 2].rearrange("p c n -> p (c n)"), ps[:, 6 + u % 2].bitcast(F16),
                             ACT.Copy).then_inc(zin_sb, 1)

            def meta_copy(i, u):
                j = RING * i + u
                act.wait_ge(rows_in[u], 16 * (i + 1))
                if not early(i, 1):
                    act.wait_ge(added, 32 * (j - RING + 1))
                a.activation(meta[:, u, :, E:E + 1], rin[:, u, :, TOK:TOK + 1], ACT.Copy).then_inc(meta_done, 1)
                a.activation(meta[:, u, :, 0:E].bitcast(F32), rin[:, u, :, COMB:COMB + E].bitcast(F32),
                             ACT.Copy).then_inc(meta_done, 1)

            def weigh(i, u):
                j = RING * i + u
                e = act.value_load(tile_exp[0:1, dyn(j)], min_val=0, max_val=E - 1)
                act.wait_ge(meta_done, 2 * (j + 1))
                if not early(j, 2):
                    act.wait_ge(added, 32 * (j - 1))
                for h in range(2):
                    act.wait_ge(yv_done, 2 * j + h + 1)
                    a.activation(y[:, u % 2, h], yv[:, h], ACT.Copy,
                                 scale=meta[:, u, h].bitcast(F32)[:, dyn(e)]).then_inc(y_done, 1)

            act.wait_ge(tables, 1)
            staged(act, NT, [(hi_part, 1), (zin_copy, 0), (meta_copy, 0), (weigh, 2)], turn=RING)

        @block.vector
        def _(dve):
            v = nc.vector

            def chain(semaphore, base, on=True):
                count = [0]

                def step(op, *args):
                    if on:
                        if count[0]:
                            dve.wait_ge(semaphore, base + count[0])
                        op(*args).then_inc(semaphore, 1)
                        count[0] += 1
                return step, count

            v.memset(pad[:], 0).then_inc(pad_out, 1)
            v.memset(kv_bd[:], 0.0).then_inc(kv_ones, 1)
            v.memset(kv[:], 1.0).then_inc(kv_ones, 1)
            dve.wait_ge(pad_out, 2)
            v.memset(pad[:, TOK:TOK + 1], T).then_inc(pad_out, 1)
            dve.wait_ge(consts, NCONST)
            dve.wait_ge(kv_ones, 2)

            def w_abs(n, kind, i):
                dve.wait_ge(w_in[kind], 16 * (i + 1))
                if not early(n, 2):
                    dve.wait_ge(wabs_all, n - 1)
                v.tensor_reduce(am[:, kind:kind + 1], stage[:, kind], AX.X, ALU.max,
                                apply_absolute_value=True).then_inc(wabs, 1)

            def w_scale(w, e, n, kind, k):
                top = wmax[:, dyn(e), kind]
                col = slice(kind, kind + 1)
                if k == 0:
                    dve.wait_ge(wabs_all, n + 1)
                    w(v.tensor_scalar, top, amr[:, col], TINY, None, ALU.max)
                elif k == 1:
                    w(v.tensor_scalar, wt[:, col].bitcast(I32), top.bitcast(I32), 23, 23,
                      ALU.logical_shift_right, ALU.logical_shift_left)
                elif k == 2:
                    w(v.tensor_scalar, winv[:, dyn(e), kind], wt[:, col], 1.0 / TOP, None, ALU.mult)
                elif k == 3:
                    w(v.tensor_scalar, am[:, col], wt[:, col], 1.0 / TOP, None, ALU.mult)
                else:
                    dve.wait_ge(wscale_s, 4 * (n + 1))
                    if not early(n, 2):
                        dve.wait_ge(whi, 2 * (n - 1))
                    v.reciprocal(wsc[:, col], am[:, col]).then_inc(wscale, 1)

            def statistics(src, j, done):
                v.bn_stats(st[:, j], src[:, j]).then_inc(done, 1)

            def aggregates(n, stats, done):
                dve.wait_ge(stats, GT * (n + 1))
                dve.sem_inc(dve_go, 1)
                for j in range(GT):
                    v.bn_aggr(mv[:, j], st[:, j]).then_inc(done, 1)

            def root(r, k, scale):
                if k == 0:
                    r(v.tensor_scalar, ve[:], mv[:, :, 1], LN_EPS, 1.0 / scale ** 2, ALU.add, ALU.mult)
                elif k == 1:
                    r(v.tensor_scalar, half[:], ve[:].bitcast(I32), 1, None, ALU.logical_shift_right)
                elif k == 2:
                    r(v.tensor_scalar, rstd[:].bitcast(I32), half[:], -1.0, float(0x5F3759DF), ALU.mult, ALU.add)
                elif k % 3 == 0:
                    r(v.tensor_tensor, nt[:, 0], rstd[:], ve[:], ALU.mult)
                elif k % 3 == 1:
                    r(v.scalar_tensor_tensor, nt[:, 1], nt[:, 0], -0.5, rstd[:], ALU.mult, ALU.mult)
                else:
                    r(v.scalar_tensor_tensor, rstd[:], nt[:, 1], 1.5, rstd[:], ALU.add, ALU.mult)

            def normalise(dst, src, j, done):
                v.tensor_scalar(dst[:, j], src[:, j], mv[:, j, 0:1], rstd[:, j:j + 1],
                                ALU.subtract, ALU.mult).then_inc(done, 1)

            def slot1(i, u, norm=True, kv_on=True, q_on=True):
                g = 2 * i + u
                ib, ub = (i, 0) if u else (i - 1, 1)
                b = g - 1
                r, _ = chain(rstd1, RSTEPS * g, norm)
                w, _ = chain(wscale_s, 4 * b, kv_on)

                def bias(j):
                    if kv_on:
                        n = GT * b + j
                        dve.wait_ge(kv_psum, n + 1)
                        if not early(b, 1):
                            dve.wait_ge(kv_sum, n - GT + 1)
                        v.tensor_tensor(kv[:, j, :, 0:D], ps[:, 4 + j % 2].rearrange("p (h d) -> p h d", d=D),
                                        bkv_sb[:], ALU.add).then_inc(kv_biased, 1)

                def k_fin(j):
                    if kv_on:
                        dve.wait_ge(k_act, 2 * (GT * b + j + 1))
                        v.scalar_tensor_tensor(kf[:, j], kexp[:, j % 2], 1.0, kf[:, j],
                                               ALU.min, ALU.add).then_inc(k_done, 1)

                def q_fin(group, par, f):
                    dve.wait_ge(q_act, 2 * (CC * group + f + 1))
                    v.scalar_tensor_tensor(qt[:, par, f], qt[:, par, f], 1.0, qrelu[:, f],
                                           ALU.min, ALU.add).then_inc(q_done, 1)

                if norm:
                    dve.wait_ge(x_in[u], 16 * (i + 1))
                    for j in range(GT):
                        statistics(xr[:, u], j, stats1)
                    if not early(g, 1):
                        dve.wait_ge(z1, GT * g)
                    aggregates(g, stats1, aggr1)
                if q_on:
                    q_fin(g - 2, u, 1)
                bias(0)
                if norm:
                    dve.wait_ge(aggr1, GT * (g + 1))
                for k in range(4):
                    root(r, k, 1.0)
                    if kv_on:
                        w_scale(w, ib, b, ub, k)
                bias(1)
                k_fin(0)
                if kv_on:
                    w_scale(w, ib, b, ub, 4)
                for k in range(4, 7):
                    root(r, k, 1.0)
                bias(2)
                k_fin(1)
                for k in range(7, RSTEPS):
                    root(r, k, 1.0)
                if norm:
                    dve.wait_ge(rstd1, RSTEPS * (g + 1))
                    if not early(g, 1):
                        dve.wait_ge(zt_psum, g)
                    normalise(z, xr[:, u], 0, z1)
                    normalise(z, xr[:, u], 1, z1)
                bias(3)
                k_fin(2)
                if norm:
                    normalise(z, xr[:, u], 2, z1)
                    normalise(z, xr[:, u], 3, z1)
                k_fin(3)
                if norm:
                    w_abs(g, u, i)
                if kv_on:
                    q_fin(b, ub, 0)

            dve.wait_ge(params_in, 16 * NPARAM)
            v.tensor_copy(ident16[:], ident[:])
            v.tensor_copy(rev[:], rev_i[:])
            v.tensor_copy(base[:], base_i[:])
            v.tensor_copy(start_row[:], base_i[:])
            v.tensor_copy(tile_no[:], tiles_i[:])
            v.tensor_scalar(low[:], low_i[:], 0, None, ALU.is_ge)
            v.tensor_reduce(b1max[:], b1_sb[:], AX.X, ALU.max, apply_absolute_value=True).then_inc(h_steps, 1)

            for k in range(4):
                slot1(k // 2, k % 2, kv_on=k > 0, q_on=k > 1)
            with dve.Fori(2, NG // 2) as i:
                slot1(i, 0)
                slot1(i, 1)
            slot1(NG // 2, 0, norm=False)
            slot1(NG // 2, 1, norm=False, kv_on=False)

            dve.wait_ge(kv_sum, GT * NG)
            for f in range(CC):
                for h in range(HB):
                    v.tensor_copy(kv_bd[h * D:(h + 1) * D, f, h * VW:(h + 1) * VW],
                                  ps[h * D:(h + 1) * D, 2 + f, h * VW:(h + 1) * VW]).then_inc(kvbd, 1)

            v.memset(msum[:].bitcast(I32), 0).then_inc(kv_ones, 1)
            v.memset(rows[:], 0).then_inc(kv_ones, 1)
            dve.wait_ge(kv_ones, 4)

            def wide(ap):
                return ap.unsqueeze(2).broadcast_to([P, GT, E])

            def slot2(i, u, attend=True, gate=True):
                g = 2 * i + u
                ib, ub = (i, 0) if u else (i - 1, 1)
                b = g - 1
                r, _ = chain(rstd2, RSTEPS * g, attend)
                c, count = chain(gate_steps, GS * b, gate)
                w, _ = chain(wscale_s, 4 * (NG + g), attend)
                nd = ps[:, 4:4 + GT, 0:NH * VW].rearrange("p j (h w) -> p j h w", w=VW)

                def divide(j):
                    if attend:
                        v.tensor_tensor(x2[:, j].rearrange("p (h d) -> p h d", d=D), nd[:, j, :, 0:D],
                                        rden[:, j].unsqueeze(2).broadcast_to([P, NH, D]), ALU.mult).then_inc(att, 1)

                if attend:
                    if not early(g, 1):
                        dve.wait_ge(att, GT * g)
                    dve.wait_ge(num_psum, GT * (g + 1))
                    v.tensor_scalar(den[:], nd[:, :, :, D], ATT_EPS, None, ALU.add).then_inc(dens, 1)
                    dve.wait_ge(dens, g + 1)
                    v.reciprocal(rden[:], den[:]).then_inc(rdens, 1)
                    if not early(g, 1):
                        dve.wait_ge(x2_out, 16 * g)
                    dve.wait_ge(rdens, g + 1)
                for j in range(GT):
                    divide(j)
                if gate:
                    ri = rows[:, ub]
                    rh = rows[:, ub].bitcast(F16)
                    dve.wait_ge(zhi, b + 1)
                    v.tensor_tensor(rh[:, :, C:2 * C], z2[:, ub], rh[:, :, 0:C], ALU.subtract).then_inc(row_data, 1)
                    v.tensor_copy(ri[:, :, TOK], tok_ids[:, dyn(b)].rearrange("p a j -> p (a j)")).then_inc(row_data, 1)
                    dve.wait_ge(logit_psum, b + 1)
                c(v.tensor_copy, lg[:], ps[:, 2, 0:GT * E].rearrange("p (j e) -> p j e", e=E))
                if attend:
                    dve.wait_ge(att, GT * (g + 1))
                    dve.wait_ge(x_in[u], 16 * (NG // 2 + i + 1))
                    v.tensor_tensor(x2[:], x2[:], xr[:, u], ALU.add).then_inc(x2_done, 1)
                c(v.tensor_reduce, mx[:, 0], lg[:], AX.X, ALU.max)
                if attend:
                    w_abs(NG + g, u, NG // 2 + i)
                c(v.tensor_tensor, eq[:], lg[:], wide(mx[:, 0]), ALU.is_equal)
                if attend:
                    dve.wait_ge(x2_done, g + 1)
                    statistics(x2, 0, stats2)
                c(v.tensor_tensor, cand[:], eq[:], rev[:], ALU.mult)
                if attend:
                    statistics(x2, 1, stats2)
                c(v.tensor_reduce, first[:], cand[:], AX.X, ALU.max)
                if attend:
                    statistics(x2, 2, stats2)
                c(v.tensor_tensor, m1[:], cand[:], wide(first[:]), ALU.is_equal)
                if attend:
                    statistics(x2, 3, stats2)
                c(v.scalar_tensor_tensor, lg2[:], m1[:], -3.0e38, lg[:], ALU.mult, ALU.add)
                if attend:
                    if not early(g, 1):
                        dve.wait_ge(z2_done, GT * g)
                    aggregates(g, stats2, aggr2)
                c(v.tensor_reduce, mx[:, 1], lg2[:], AX.X, ALU.max)
                if attend:
                    dve.wait_ge(aggr2, GT * (g + 1))
                root(r, 0, ZSCALE)
                c(v.tensor_tensor, eq[:], lg2[:], wide(mx[:, 1]), ALU.is_equal)
                root(r, 1, ZSCALE)
                c(v.tensor_tensor, cand[:], eq[:], rev[:], ALU.mult)
                root(r, 2, ZSCALE)
                c(v.tensor_reduce, first[:], cand[:], AX.X, ALU.max)
                root(r, 3, ZSCALE)
                c(v.tensor_tensor, wts[:, 0], mx[:, 1], mx[:, 0], ALU.subtract)
                assert count[0] in (0, GAP_AT)
                root(r, 4, ZSCALE)
                c(v.tensor_tensor, m2[:], cand[:], wide(first[:]), ALU.is_equal)
                root(r, 5, ZSCALE)
                c(v.tensor_tensor, msum[:, 0:GT], m1[:], m2[:], ALU.add)
                for k in range(5):
                    root(r, 6 + k, ZSCALE)
                    if attend:
                        w_scale(w, i + NG // 2, NG + g, u, k)
                root(r, 11, ZSCALE)
                if gate:
                    dve.wait_ge(gap_exp, b + 1)
                c(v.tensor_scalar, wts[:, 2], wts[:, 1], 1.0, None, ALU.add)
                if attend:
                    dve.wait_ge(rstd2, RSTEPS * (g + 1))
                    if not early(i, 1):
                        dve.wait_ge(row_data, 3 * (g - 1))
                        dve.wait_ge(z2t_psum, g - 1)
                    normalise(z2[:, u], x2, 0, z2_done)
                c(v.reciprocal, wts[:, 3], wts[:, 2])
                if attend:
                    normalise(z2[:, u], x2, 1, z2_done)
                c(v.tensor_tensor, wts[:, 4], wts[:, 1], wts[:, 3], ALU.mult)
                if attend:
                    normalise(z2[:, u], x2, 2, z2_done)
                    normalise(z2[:, u], x2, 3, z2_done)
                if not gate:
                    return
                c(v.tensor_tensor, cb[:, 0], m1[:], wide(wts[:, 3]), ALU.mult)
                c(v.tensor_tensor, cb[:, 1], m2[:], wide(wts[:, 4]), ALU.mult)
                dve.wait_ge(rank_psum, b + 1)
                ranks = ps[:, 3, 0:(GT + 1) * E].rearrange("p (j e) -> p j e", e=E)
                c(v.tensor_tensor, pos[:], ranks[:, 0:GT], base[:].unsqueeze(1).broadcast_to([P, GT, E]), ALU.add)
                v.tensor_tensor(rows[:, ub].bitcast(F32)[:, :, COMB:COMB + E], cb[:, 0], cb[:, 1],
                                ALU.add).then_inc(row_data, 1)
                c(v.tensor_tensor, base[:], base[:], ranks[:, GT], ALU.add)
                assert count[0] == GS
                v.tensor_tensor(pos1[:], m1[:], pos[:], ALU.mult).then_inc(pl_steps, 1)
                v.tensor_tensor(eq[:], m2[:], pos[:], ALU.mult).then_inc(pl_steps, 1)
                if not early(ib, 1):
                    dve.wait_ge(scattered[ub], 16 * 2 * GT * ib)
                dve.wait_ge(pl_steps, 3 * b + 2)
                v.tensor_reduce(idx[:, ub, 0], pos1[:], AX.X, ALU.add).then_inc(pl_steps, 1)
                dve.wait_ge(pl_steps, 3 * b + 3)
                v.tensor_reduce(idx[:, ub, 1], eq[:], AX.X, ALU.add).then_inc(placed, 1)
                dve.wait_ge(gate_steps, GS * (b + 1))

            for k in range(4):
                slot2(k // 2, k % 2, gate=k > 0)
            with dve.Fori(2, NG // 2) as i:
                slot2(i, 0)
                slot2(i, 1)
            slot2(NG // 2, 0, attend=False)

            step, count = chain(tab_steps, 0)
            step(v.tensor_copy, pad_row[:], base[0:1])
            step(v.tensor_tensor, ends[:], base[0:1], start_row[0:1], ALU.subtract)
            step(v.tensor_scalar, cnt_i[:, 0], ends[:], float(TS - 1), None, ALU.add)
            step(v.tensor_scalar, cnt_i[:, 1], cnt_i[:, 0], TS.bit_length() - 1, None, ALU.logical_shift_right)
            step(v.tensor_copy, ntile[:], cnt_i[:, 1])
            step(v.tensor_tensor, ends3[:], low[:], ntile[:].unsqueeze(1).broadcast_to([1, E, E]), ALU.mult)
            step(v.tensor_reduce, ends[:], ends3[:], AX.X, ALU.add)
            step(v.tensor_tensor, past[:], tile_no[:].unsqueeze(2).broadcast_to([1, NT, E]),
                                 ends[:].unsqueeze(1).broadcast_to([1, NT, E]), ALU.is_ge)
            step(v.tensor_reduce, tab_f[:, 0], past[:], AX.X, ALU.add)
            step(v.tensor_tensor, past_n[:], past[:], ntile[:].unsqueeze(1).broadcast_to([1, NT, E]), ALU.mult)
            step(v.tensor_reduce, tab_f[:, 1], past_n[:], AX.X, ALU.add)
            step(v.tensor_tensor, tab_f[:, 2], tile_no[:], tab_f[:, 1], ALU.subtract)
            step(v.tensor_scalar, tab_f[:, 3], tab_f[:, 0], float(CAP), None, ALU.mult)
            step(v.scalar_tensor_tensor, tile_row[:], tab_f[:, 2], float(TS), tab_f[:, 3], ALU.mult, ALU.add)
            step(v.tensor_scalar, tile_exp[:], tab_f[:, 0], float(E - 1), None, ALU.min)

            dve.wait_ge(b1_all, 1)
            step(v.scalar_tensor_tensor, htmp[:, 0], wmax[:, :, 0], float(C) ** 0.5 * ZBOUND, b1maxr[:], ALU.mult, ALU.add)
            step(v.tensor_scalar, htmp[:, 1].bitcast(I32), htmp[:, 0].bitcast(I32), 23, 23,
                                 ALU.logical_shift_right, ALU.logical_shift_left)
            step(v.tensor_scalar, hinv[:], htmp[:, 1], 1.0 / TOP, None, ALU.mult)
            step(v.reciprocal, hscale[:], hinv[:])
            step(v.scalar_tensor_tensor, l1_scale[:], hscale[:], 1.0 / ZSCALE, winv[:, :, 0], ALU.mult, ALU.mult)
            step(v.tensor_tensor, y_scale[:], hinv[:], winv[:, :, 1], ALU.mult)
            step(v.tensor_tensor, b1s[:], b1_sb[:], hscale[:].unsqueeze(2).broadcast_to([P, E, HC]), ALU.mult)
            v.memset(htmp[:], 0.0).then_inc(tables, 1)

            def y_part(i, u, h, e):
                j = RING * i + u
                if h == 0:
                    dve.wait_ge(l2_psum, j + 1)
                if not early(j, 1):
                    dve.wait_ge(y_done, 2 * (j - 1) + h + 1)
                v.scalar_tensor_tensor(yu[:, h], ps[:, 4 + h, 0:C], y_scale[:, dyn(e)],
                                       b2_sb[:, dyn(e)].rearrange("p a c -> p (a c)"), ALU.mult, ALU.add).then_inc(yu_done, 1)
                dve.wait_ge(yu_done, 2 * j + h + 1)
                v.scalar_tensor_tensor(yv[:, h], ps[:, 4 + h, C:2 * C], y_scale[:, dyn(e)], yu[:, h],
                                       ALU.mult, ALU.add).then_inc(yv_done, 1)

            def hidden(i, u):
                j = RING * i + u
                e = dve.value_load(tile_exp[0:1, dyn(j)], min_val=0, max_val=E - 1)

                def scaled(k):
                    dve.wait_ge(l1_psum, 4 * j + k + 1)
                    if not early(j, 1):
                        dve.wait_ge(lo_done, 4 * (j - 1) + k + 1)
                    v.scalar_tensor_tensor(
                        hx[:, k].rearrange("p (h n) -> p h n", h=2), ps[:, k].rearrange("p (h n) -> p h n", h=2),
                        l1_scale[:, dyn(e)],
                        b1s[:, dyn(e), 2 * k:2 * k + 2].rearrange("p a h -> p (a h)").unsqueeze(2).broadcast_to([P, 2, TS]),
                        ALU.mult, ALU.add).then_inc(hx_done, 1)

                def lo_part(k):
                    dve.wait_ge(hi_done, 4 * j + k + 1)
                    v.scalar_tensor_tensor(
                        hlo[:, u % 2, 2 * k:2 * k + 2].rearrange("p h n -> p (h n)"), hx[:, k], 0.0,
                        hhi[:, u % 2, 2 * k:2 * k + 2].rearrange("p h n -> p (h n)"), ALU.max, ALU.subtract).then_inc(lo_done, 1)

                if not early(j, 2):
                    dve.wait_ge(l2_psum, j - 1)
                scaled(0)
                scaled(1)
                lo_part(0)
                scaled(2)
                lo_part(1)
                scaled(3)
                lo_part(2)
                lo_part(3)

            def result(i, u):
                e = dve.value_load(tile_exp[0:1, dyn(RING * i + u)], min_val=0, max_val=E - 1)
                if early(RING * i + u, 1):
                    dve.wait_ge(b2_in, 16)
                y_part(i, u, 0, e)
                y_part(i, u, 1, e)

            dve.wait_ge(tables, 1)
            dve.wait_ge(wlo, 2 * NG)
            for u in range(2):
                dve.wait_ge(scattered[u], 16 * GT * NG)
            dve.wait_ge(x2_out, 16 * NG)
            staged(dve, NT, [(hidden, 1), (result, 2)], turn=RING)

        @block.tensor
        def _(pe):
            t = nc.tensor
            pe.wait_ge(consts, NCONST)
            pe.wait_ge(params_in, 16 * NPARAM)

            def turn(src, i, u, ready, psum_read, done):
                g = 2 * i + u
                pe.wait_ge(ready, GT * (g + 1))
                if not early(g, 1):
                    pe.wait_ge(psum_read, g)
                for c in range(CC):
                    for j in range(GT):
                        ins = t.transpose(ps[:, c, j * P:(j + 1) * P], src[:, j, c * P:(c + 1) * P], ident[:])
                ins.then_inc(done, 1)

            def project(i, u, part):
                g = 2 * i + u
                if part == 0:
                    pe.wait_ge(zt_sb, g + 1)
                head = early(g, 1)
                tail = isinstance(g, int) and g == NG - 1

                def proj(j):
                    n = GT * g + j
                    if not early(n, 2):
                        pe.wait_ge(kv_biased, n - 1)
                    for c in range(CC):
                        ins = t.matmul(ps[:, 4 + j % 2], zT[:, u, c, j * P:(j + 1) * P],
                                       wkv_sb[:, c].rearrange("p k n -> p (k n)"), start=(c == 0), stop=(c == CC - 1))
                    ins.then_inc(kv_psum, 1)

                def add_kv(j):
                    pe.wait_ge(k_done, GT * g + j + 1)
                    for f in range(CC):
                        ins = t.matmul(ps[:, 2 + f, 0:NHC], kf[:, j, f * P:(f + 1) * P],
                                       kv[:, j, NH + f * HB:NH + (f + 1) * HB].rearrange("p h w -> p (h w)"),
                                       start=(head and j == 0), stop=(tail and j == GT - 1))
                    ins.then_inc(kv_sum, 1)

                def q_chunk(f):
                    if not head:
                        pe.wait_ge(q_act, 2 * (CC * (g - 1) + f + 1))
                    for c in range(CC):
                        ins = t.matmul(ps[:, 6 + f], wq_sb[:, c, f * P:(f + 1) * P], zT[:, u, c],
                                       start=(c == 0), stop=(c == CC - 1))
                    ins.then_inc(q_psum, 1)

                if part == 0:
                    proj(0)
                    proj(1)
                    proj(2)
                    add_kv(0)
                    proj(3)
                    add_kv(1)
                    q_chunk(0)
                    add_kv(2)
                else:
                    add_kv(3)
                    q_chunk(1)

            staged(pe, NG, [(lambda i, u: project(i, u, 0), 1), (lambda i, u: turn(z, i, u, z1, zt_sb, zt_psum), 0),
                            (lambda i, u: project(i, u, 1), 1)])

            pe.wait_ge(kvbd, CC * HB)

            def numerators(i, u):
                g = 2 * i + u
                pe.wait_ge(qt_in[u], 16 * (i + 1))
                for j in range(GT):
                    if not early(g, 1):
                        pe.wait_ge(att, GT * (g - 1) + j + 1)
                    for f in range(CC):
                        ins = t.matmul(ps[:, 4 + j, f * NHC:(f + 1) * NHC], qt[:, u, f, j * P:(j + 1) * P],
                                       kv_bd[:, f], start=True, stop=True)
                    ins.then_inc(num_psum, 1)

            def logits(i, u):
                g = 2 * i + u
                pe.wait_ge(z2t_sb, g + 1)
                if not early(g, 1):
                    pe.wait_ge(gate_steps, GS * (g - 1) + 1)
                for j in range(GT):
                    for c in range(CC):
                        ins = t.matmul(ps[:, 2, j * E:(j + 1) * E], zT[:, u, c, j * P:(j + 1) * P], gw_sb[:, c],
                                       start=(c == 0), stop=(c == CC - 1))
                ins.then_inc(logit_psum, 1)

            def rank(i, u):
                g = 2 * i + u
                pe.wait_ge(gate_steps, GS * g + GAP_AT + 2)
                t.matmul(ps[:, 3, 0:(GT + 1) * E], tri[:], msum[:].rearrange("p j e -> p (j e)"), start=True, stop=False)
                for j in range(GT):
                    ins = t.matmul(ps[:, 3, (j + 1) * E:(GT + 1) * E].rearrange("p (k e) -> p k e", e=E), ones[:],
                                   msum[:, j].unsqueeze(1).broadcast_to([P, GT - j, E]),
                                   start=False, stop=(j == GT - 1))
                ins.then_inc(rank_psum, 1)

            staged(pe, NG, [(lambda i, u: turn(z2[:, u], i, u, z2_done, z2t_sb, z2t_psum), 2), (logits, 2),
                            (numerators, 0), (rank, 2)])

            pe.wait_ge(tables, 1)

            def layer1(i, u):
                j = RING * i + u
                e = pe.value_load(tile_exp[0:1, dyn(j)], min_val=0, max_val=E - 1)
                if early(j, 1):
                    pe.wait_ge(wlo, 2 * NG)
                pe.wait_ge(zin_sb, j + 1)
                for k in range(4):
                    if not early(j, 1):
                        pe.wait_ge(hx_done, 4 * (j - 1) + k + 1)
                    for h in range(2):
                        col = (2 * k + h) * P
                        n = 0
                        for c in range(CC):
                            whi_ap = w1s[:, dyn(e), 0, c * HC * P + col:c * HC * P + col + P].rearrange("p a n -> p (a n)")
                            wlo_ap = w1s[:, dyn(e), 1, c * HC * P + col:c * HC * P + col + P].rearrange("p a n -> p (a n)")
                            for w, zz in ((whi_ap, c), (whi_ap, CC + c), (wlo_ap, c)):
                                ins = t.matmul(ps[:, k, h * TS:(h + 1) * TS], w, zin[:, u % 2, zz],
                                               start=(n == 0), stop=(n == 3 * CC - 1))
                                n += 1
                    ins.then_inc(l1_psum, 1)

            def layer2(i, u):
                j = RING * i + u
                e = pe.value_load(tile_exp[0:1, dyn(j)], min_val=0, max_val=E - 1)
                if not early(j, 1):
                    pe.wait_ge(yv_done, 2 * j)
                for c in range(HC):
                    if c % 2 == 0:
                        pe.wait_ge(lo_done, 4 * j + c // 2 + 1)
                    both = w2s[:, dyn(e), c].rearrange("p a k n -> p (a k n)")
                    high = w2s[:, dyn(e), c, 0].rearrange("p a n -> p (a n)")
                    for h in range(2):
                        t.matmul(ps[:, 4 + h], hhi[:, u % 2, c, h * P:(h + 1) * P], both, start=(c == 0), stop=False)
                    for h in range(2):
                        ins = t.matmul(ps[:, 4 + h, C:2 * C], hlo[:, u % 2, c, h * P:(h + 1) * P], high,
                                       start=False, stop=(c == HC - 1))
                ins.then_inc(l2_psum, 1)

            def turn_rows(i, u):
                pe.wait_ge(rows_in[u], 16 * (i + 1))
                if not early(RING * i + u, 2):
                    pe.wait_ge(zin_sb, RING * i + u - 1)
                for c in range(2 * CC):
                    for h in range(2):
                        ins = t.transpose(ps[:, 6 + u % 2].bitcast(F16)[:, c * TS + h * P:c * TS + (h + 1) * P],
                                          rin[:, u, h].bitcast(F16)[:, c * P:(c + 1) * P], ident16[:])
                ins.then_inc(zin_psum, 1)

            staged(pe, NT, [(layer1, 1), (turn_rows, 0), (layer2, 2)], turn=RING)


def kernel(**inputs):
    import numpy as _np
    import concourse.bacc as _bacc
    from concourse import mybir as _mybir
    from concourse.bass_utils import run_bass_kernel_spmd as _run

    a = {k: _np.asarray(v) for k, v in inputs.items()}
    B, L, C = a["L0_attn_x"].shape
    E, HID, _ = a["L0_ffn_w1"].shape
    cc, hc = C // 128, HID // 128

    def rows_first(w):
        return w.reshape(cc, 128, -1).transpose(1, 0, 2)

    arrays = {
        "x": a["L0_attn_x"].reshape(B * L, C),
        "wq": rows_first(a["L0_attn_Wq"]), "bq": a["L0_attn_bq"].reshape(cc, 128).T,
        "wk": rows_first(a["L0_attn_Wk"]), "bk": a["L0_attn_bk"],
        "wv": rows_first(a["L0_attn_Wv"]), "bv": a["L0_attn_bv"],
        "gate_w": rows_first(a["L0_ffn_gate_w"].T),
        "w1": a["L0_ffn_w1"].reshape(E, HID, cc, 128).transpose(0, 3, 2, 1).reshape(E, 128, cc * HID),
        "b1": a["L0_ffn_b1"].reshape(E, hc, 128).transpose(2, 0, 1),
        "w2": a["L0_ffn_w2"].reshape(E, C, hc, 128).transpose(0, 3, 2, 1).reshape(E, 128, hc * C),
        "b2": a["L0_ffn_b2"].reshape(E * C),
    }
    arrays = {k: _np.ascontiguousarray(v) for k, v in arrays.items()}
    nc = _bacc.Bacc("TRN2", target_bir_lowering=False, num_devices=1)
    args = [nc.dram_tensor(k, v.shape, _mybir.dt.from_np(v.dtype), kind="ExternalInput").ap()
            for k, v in arrays.items()]
    out = nc.dram_tensor("out", (B * L, C), _mybir.dt.float32, kind="ExternalOutput").ap()
    attention_moe(nc, *args, out)
    r = _run(nc, [arrays], core_ids=[0])
    return r.results[0]["out"].reshape(B, L, C)
```

```python
from contextlib import ExitStack

import concourse.bass as bass
from concourse import mybir

ALU = mybir.AluOpType
ACT = mybir.ActivationFunctionType
AX = mybir.AxisListType
F32 = mybir.dt.float32
F16 = mybir.dt.float16
I32 = mybir.dt.int32
BF16 = mybir.dt.bfloat16
RMAX = bass.bass_isa.ReduceOp.max

P = 128
GT = 4
LN_EPS = 1e-5
ATT_EPS = 1e-6
ZBOUND = 16.0
ZSCALE = 1024.0
TOP = 2.0 ** 14
TINY = 1e-12
SQ = 2.0 ** -20


def dyn(i, n=1):
    return bass.DynSlice(i, n)


def early(number, count):
    return isinstance(number, int) and number < count


def staged(eng, n, steps, turn=2, alike=None):
    alike = alike or n
    lags = max(lag for _, lag in steps)

    def slot(i, u, number=None):
        for f, lag in steps:
            if number is None or lag <= number < n + lag:
                back = -((u - lag) // turn)
                f(i - back if back else i, (u - lag) % turn)
    for k in range(4):
        slot(k // turn, k % turn, k)
    with eng.Fori(4 // turn, alike // turn) as i:
        for u in range(turn):
            slot(i, u)
    for k in range(alike // turn * turn, n + lags):
        slot(k // turn, k % turn, k)


def attention_moe(nc, x, wq, bq, wk, bk, wv, bv, gate_w, w1, b1, w2, b2, out):
    T, C = x.shape
    E = gate_w.shape[2]
    HC = b1.shape[2]
    CC = C // P
    NH = 8
    D = C // NH
    HB = P // D
    NG = T // (GT * P)
    TS = 2 * P
    PAIRS, SINGLES = 2 * T // TS, E
    NT = PAIRS + SINGLES
    CAP = T + P
    ROW = C + 16
    COMB, TOK = C, C + E
    assert PAIRS % 4 == 0
    RING = 4
    VW = D + 1
    NHC = HB * VW
    PIECE = HC * C
    assert 2 * E == 2 * NG and NG % 2 == 0

    scratch = nc.dram_tensor("rows_by_expert", [E * CAP + TS, ROW], I32, kind="Internal").ap()
    qt_dram = nc.dram_tensor("q_transposed", [NG, P, CC * GT * P], F32, kind="Internal").ap()
    x_v = x.rearrange("(g p j) c -> g p (j c)", p=P, j=GT)
    out_v = out.rearrange("(g p j) c -> g p (j c)", p=P, j=GT)

    with ExitStack() as ctx:
        def sb(name, shape, dt=F32, scope=ctx):
            return scope.enter_context(nc.sbuf_tensor(name, shape, dt))

        def sem(name):
            return ctx.enter_context(nc.semaphore(name))

        ps = ctx.enter_context(nc.psum_tensor("ps", [P, 8, 512], F32))
        w1s = sb("w1_split", [P, E, 2, CC * HC, P], F16)
        w2s = sb("w2_split", [P, E, HC, 2, C], F16)
        ident = sb("ident", [P, P])
        tri = sb("tri", [P, P], F16)
        ones = sb("ones", [P, P], F16)
        ident16 = sb("ident16", [P, P], F16)
        wkv_sb = sb("wkv_sb", [P, CC, 2, C])
        bq_sb = sb("bq_sb", [P, CC])
        gw_sb = sb("gw_sb", [P, CC, E])
        b1_sb = sb("b1_sb", [P, E, HC])
        b1s = sb("b1_scaled", [P, E, HC])
        kv_bd = sb("kv_blockdiag", [P, CC, NHC])
        pad = sb("pad_rows", [P, ROW], I32)
        tok_ids = sb("tok_ids", [P, NG, GT], I32)
        winv = sb("winv", [P, E, 2])
        b1max = sb("b1max", [P, E])
        b1maxr = sb("b1maxr", [P, E])
        hscale = sb("hscale", [P, E])
        hinv = sb("hinv", [P, E])
        htmp = sb("htmp", [P, 2, E])
        l1_scale = sb("l1_scale", [P, E])
        y_scale = sb("y_scale", [P, E])
        am = sb("am", [P, 2])
        amr = sb("amr", [P, 2])
        wt = sb("wt", [P, 2])
        wsc = sb("wsc", [P, 2])
        rev = sb("rev", [P, GT, E])
        base = sb("base", [P, E])
        start_row = sb("start_row", [P, E])
        tile_no = sb("tile_no", [1, NT])
        low = sb("low", [1, E, E])
        cnt_i = sb("cnt_i", [1, 3, E], I32)
        counts = sb("counts", [1, 4, E])
        nsingle = sb("nsingle", [1, E])
        ends = sb("ends", [1, 2, E + 1])
        ends3 = sb("ends3", [1, E, E])
        origin = sb("origin", [1, 2, E + 1])
        pad_row = sb("pad_row", [1, E], I32)
        tile_row = sb("tile_row", [1, NT], I32)
        tile_exp = sb("tile_exp", [1, NT], I32)

        s12 = ExitStack()
        xr = sb("x_ring", [P, 2, GT, C], scope=s12)
        qt = sb("qt_ring", [P, 2, CC, GT * P], scope=s12)
        stage = sb("w_stage", [P, 2, PIECE], scope=s12)
        st = sb("bn_st", [P, GT, 6], scope=s12)
        mv = sb("mean_var", [P, GT, 2], scope=s12)
        rstd = sb("rstd", [P, GT], scope=s12)
        ve = sb("ve", [P, GT], scope=s12)
        half = sb("half", [P, GT], I32, scope=s12)
        nt = sb("newton", [P, 2, GT], scope=s12)
        zT = sb("zT", [P, 2, CC, GT * P], scope=s12)
        s1 = ExitStack()
        wq_sb = sb("wq_sb", [P, CC, C], scope=s1)
        bkv_sb = sb("bkv_sb", [P, 2 * NH, D], scope=s1)
        z = sb("z", [P, GT, C], scope=s1)
        kv = sb("kv", [P, GT, 2 * NH, VW], scope=s1)
        kf = sb("kf", [P, GT, C], scope=s1)
        s0 = ExitStack()
        rev_i = sb("rev_i", [P, GT, E], I32, scope=s0)
        base_i = sb("base_i", [P, E], I32, scope=s0)
        tiles_i = sb("tiles_i", [1, NT], I32, scope=s0)
        low_i = sb("low_i", [1, E, E], I32, scope=s0)
        s0.close()
        kexp = sb("kexp", [P, 2, C], scope=s1)
        qrelu = sb("qrelu", [P, CC, GT * P], scope=s1)
        s1.close()
        x2 = sb("x2", [P, 2, GT, C], scope=s12)
        shift = sb("shift", [P, GT], scope=s12)
        rows = sb("rows", [P, 2, GT, ROW], I32, scope=s12)
        den = sb("den", [P, GT, NH], scope=s12)
        rden = sb("rden", [P, GT, NH], scope=s12)
        lg2 = sb("lg2", [P, GT, E], scope=s12)
        eq = sb("eq", [P, GT, E], scope=s12)
        cand = sb("cand", [P, GT, E], scope=s12)
        mx = sb("mx", [P, 2, GT], scope=s12)
        first = sb("first", [P, GT], scope=s12)
        chosen = sb("chosen", [P, 2, GT, E], scope=s12)
        msum = sb("msum", [P, GT + 1, E], F16, scope=s12)
        wts = sb("wts", [P, 5, GT], scope=s12)
        cb = sb("cb", [P, 2, GT, E], scope=s12)
        pos = sb("pos", [P, GT, E], scope=s12)
        pos2 = sb("pos2", [P, 2, GT, E], scope=s12)
        idx = sb("idx", [P, 2, 2, GT], I32, scope=s12)
        past = [sb(f"past{k}", [1, n, E + 2], scope=s12) for k, n in enumerate((PAIRS, SINGLES))]
        here = [sb(f"here{k}", [1, n, E + 1], scope=s12) for k, n in enumerate((PAIRS, SINGLES))]
        where = [sb(f"where{k}", [1, 2, n], scope=s12) for k, n in enumerate((PAIRS, SINGLES))]
        s12.close()
        rin = sb("rin", [P, RING, 2, ROW], I32)
        zsplit = sb("zsplit", [P, 2, 2, 2 * C], F16)
        zin = sb("zin", [P, 2, 2 * CC, TS], F16)
        meta = sb("meta", [P, RING, 2, 16], I32)
        hx = sb("hx", [P, 4, 2, TS])
        hhi = sb("hhi", [P, 2, HC, TS], F16)
        hlo = sb("hlo", [P, 2, HC, TS], F16)
        b2_sb = sb("b2_sb", [P, E, C])
        yu = sb("yu", [P, 2, C])
        yv = sb("yv", [P, 2, C])
        y = sb("y", [P, 2, 2, C])

        names = """consts kv_ones pad_out spare_out b2_in
            stats1 aggr1 rstd1 z1 zt_psum zt_sb q_psum q_act q_done kv_psum kv_biased k_act k_done kv_sum
            kvbd wabs wabs_all wscale_s wscale whi wlo
            num_psum dens rdens att x2_done stats2 aggr2 rstd2 z2_done z2t_psum z2t_sb row_data
            logit_psum gate_steps gap_exp rank_psum placed pl_steps
            h_steps h_scales b1_all tab_steps tab_p tab_s tables pads_out
            l1_psum hx_done hi_done lo_done l2_psum yu_done yv_done y_done added""".split()
        s = {n: sem(n) for n in names}
        (consts, kv_ones, pad_out, spare_out, b2_in,
         stats1, aggr1, rstd1, z1, zt_psum, zt_sb, q_psum, q_act, q_done, kv_psum, kv_biased, k_act,
         k_done, kv_sum, kvbd, wabs, wabs_all, wscale_s, wscale, whi, wlo,
         num_psum, dens, rdens, att, x2_done, stats2, aggr2, rstd2, z2_done, z2t_psum, z2t_sb,
         row_data, logit_psum, gate_steps, gap_exp, rank_psum, placed, pl_steps,
         h_steps, h_scales, b1_all, tab_steps, tab_p, tab_s, tables, pads_out,
         l1_psum, hx_done, hi_done, lo_done, l2_psum, yu_done, yv_done, y_done, added) = (s[n] for n in names)
        params_in = sem("params_in")
        q_min = sem("q_min")
        x_in = [sem("x_in0"), sem("x_in1")]
        w_in = [sem("w_in0"), sem("w_in1")]
        qt_out = [sem("qt_out0"), sem("qt_out1")]
        qt_in = [sem("qt_in0"), sem("qt_in1")]
        x2_out = [sem("x2_out0"), sem("x2_out1")]
        scattered = [sem("scattered0"), sem("scattered1")]
        rows_in = [sem(f"rows_in{u}") for u in range(RING)]
        zhi, zlo, zin_psum, zin_sb, meta_done = (sem(n) for n in ("zhi", "zlo", "zin_psum", "zin_sb", "meta_done"))
        NPARAM = 8
        NCONST = 9
        pool_go, dve_go, act_go = sem("pool_go"), sem("dve_go"), sem("act_go")

        RSTEPS = 12
        GS, GAP_AT = 19, 11
        ctx.enter_context(nc.allow_low_precision(reason="row numbers, summed in float32 into int32, are exact"))

        def last_group(i, u):
            return isinstance(i, int) and 2 * i + u == NG - 1

        def halves(j):
            return 1 if isinstance(j, int) and j >= PAIRS else 2

        def granules(j):
            return PAIRS + j if isinstance(j, int) and j >= PAIRS else 2 * j

        held = {}

        def expert_of(eng, name, j):
            if not (isinstance(j, int) and j >= PAIRS):
                return eng.value_load(tile_exp[0:1, dyn(j)], min_val=0, max_val=E - 1)
            if (name, j) not in held:
                held[name, j] = eng.value_load(tile_exp[0:1, dyn(j)], min_val=0, max_val=E - 1)
            return held[name, j]

        block = ctx.enter_context(nc.Block())

        @block.sync
        def _(sp):
            def load_w(i, kind):
                src = (w1 if kind == 0 else w2)[dyn(i)].rearrange("a p n -> p (a n)")
                sp.dma_start(stage[:, kind], src).then_inc(w_in[kind], 16)

            sp.dma_start(xr[:, 0].rearrange("p j c -> p (j c)"), x_v[0]).then_inc(x_in[0], 16)
            sp.dma_start(wkv_sb[:, :, 0], wk).then_inc(params_in, 16)
            sp.dma_start(wkv_sb[:, :, 1], wv).then_inc(params_in, 16)
            sp.dma_start(bkv_sb[:, 0:NH].rearrange("p h d -> p (h d)"), bk.partition_broadcast(P)).then_inc(params_in, 16)
            sp.dma_start(bkv_sb[:, NH:].rearrange("p h d -> p (h d)"), bv.partition_broadcast(P)).then_inc(params_in, 16)
            sp.dma_start(wq_sb[:], wq).then_inc(params_in, 16)
            sp.dma_start(bq_sb[:], bq).then_inc(params_in, 16)
            sp.dma_start(gw_sb[:], gate_w).then_inc(params_in, 16)
            sp.dma_start(b1_sb[:], b1).then_inc(params_in, 16)
            load_w(0, 0)
            sp.dma_start(xr[:, 1].rearrange("p j c -> p (j c)"), x_v[1]).then_inc(x_in[1], 16)
            load_w(0, 1)
            sp.wait_ge(pad_out, 3)
            sp.dma_start(scratch[E * CAP:E * CAP + TS].rearrange("(p s) r -> p s r", p=P),
                         pad[:].unsqueeze(1).broadcast_to([P, TS // P, ROW])).then_inc(spare_out, 16)

            def load_x(i, u):
                if not early(i, 1):
                    sp.wait_ge(z1, GT * (2 * i + u - 1))
                    sp.dma_start(xr[:, u].rearrange("p j c -> p (j c)"),
                                 x_v[dyn(2 * i + u)].rearrange("a p n -> p (a n)")).then_inc(x_in[u], 16)

            H2 = NG // 2

            def load_x2(i, u):
                g = 2 * i + u
                if early(i, 1):
                    sp.wait_ge(z1, GT * (NG - 1 + u))
                else:
                    sp.wait_ge(x2_done, g - 1)
                sp.dma_start(xr[:, u].rearrange("p j c -> p (j c)"),
                             x_v[dyn(g)].rearrange("a p n -> p (a n)")).then_inc(x_in[u], 16)

            def load_q(i, u):
                g = 2 * i + u
                sp.wait_ge(qt_out[u], 16 * H2)
                if not early(i, 1):
                    sp.wait_ge(num_psum, GT * (g - 1))
                sp.dma_start(qt[:, u].rearrange("p c n -> p (c n)"),
                             qt_dram[dyn(g)].rearrange("a p n -> p (a n)")).then_inc(qt_in[u], 16)

            def load_w2(i, u):
                sp.wait_ge(wlo, NG + 2 * i + u - 1)
                load_w(i + H2, u)

            def store_q(i, u):
                if last_group(i, u):
                    load_x2(0, 0)
                    load_q(0, 0)
                    load_w2(0, 0)
                    load_x2(0, 1)
                sp.wait_ge(q_done, CC * (2 * i + u + 1))
                sp.dma_start(qt_dram[dyn(2 * i + u)].rearrange("a p n -> p (a n)"),
                             qt[:, u].rearrange("p c n -> p (c n)")).then_inc(qt_out[u], 16)

            def load_w1(i, u):
                if not early(i, 1):
                    sp.wait_ge(wlo, 2 * i + u - 1)
                    load_w(i, u)

            staged(sp, NG, [(load_x, 0), (load_w1, 1), (store_q, 3)])

            def store_x2(i, u):
                sp.wait_ge(x2_done, 2 * i + u + 1)
                sp.dma_start(out_v[dyn(2 * i + u)].rearrange("a p n -> p (a n)"),
                             x2[:, u].rearrange("p j c -> p (j c)")).then_inc(x2_out[u], 16)

            def load2(i, u):
                if not early(2 * i + u, 2):
                    load_x2(i, u)
                if not early(2 * i + u, 1):
                    load_q(i, u)

            staged(sp, NG, [(load2, 0), (store_x2, 2),
                            (lambda i, u: None if early(2 * i + u, 1) else load_w2(i, u), 1)])

            sp.wait_ge(tab_steps, 1)
            for e in range(E):
                r = sp.value_load(pad_row[0:1, e:e + 1], min_val=0, max_val=E * CAP - P)
                sp.dma_start(scratch[dyn(r, P)], pad[:]).then_inc(pads_out, 16)
            sp.wait_ge(tables, 1)
            sp.wait_ge(spare_out, 16)
            sp.wait_ge(pads_out, 16 * E)
            for u in range(2):
                sp.wait_ge(scattered[u], 16 * GT * NG)

            def load_rows(i, u):
                j = RING * i + u
                if early(i, 1) and u == 2:
                    sp.wait_ge(wlo, 2 * NG)
                    for k in range(2):
                        sp.wait_ge(x2_out[k], 8 * NG)
                    sp.dma_start(b2_sb[:].rearrange("p e c -> p (e c)"), b2.partition_broadcast(P)).then_inc(b2_in, 16)
                r = sp.value_load(tile_row[0:1, dyn(j)], min_val=0, max_val=E * CAP)
                if not early(i, 1):
                    sp.wait_ge(meta_done, 2 * (j - RING + 1))
                H = halves(j)
                sp.dma_start(rin[:, u, 0:H].rearrange("p h r -> p (h r)"),
                             scratch[dyn(r, H * P)].rearrange("(p h) r -> p (h r)", p=P)).then_inc(rows_in[u], 16)

            staged(sp, NT, [(load_rows, 0)], turn=RING, alike=PAIRS)

        @block.gpsimd
        def _(pool):
            g = nc.gpsimd
            g.memset(ident[:], 0.0).then_inc(consts, 1)
            g.memset(tri[:], 1.0).then_inc(consts, 1)
            g.memset(ones[:], 1.0).then_inc(consts, 1)
            g.memset(kv[:].rearrange("p j h w -> p (j h) w")[:, :, D:VW], 1.0).then_inc(kv_ones, 1)
            pool.wait_ge(consts, 3)
            g.affine_select(out=ident[:], in_=ident[:], compare_op=ALU.not_equal, fill=1.0, base=0,
                            pattern=[[-1, P]], channel_multiplier=1).then_inc(consts, 1)
            g.affine_select(out=tri[:], in_=tri[:], compare_op=ALU.is_gt, fill=0.0, base=0,
                            pattern=[[1, P]], channel_multiplier=-1).then_inc(consts, 1)
            g.iota(rev_i[:], pattern=[[0, GT], [-1, E]], base=E, channel_multiplier=0).then_inc(consts, 1)
            g.iota(base_i[:], pattern=[[CAP, E]], base=0, channel_multiplier=0).then_inc(consts, 1)
            g.iota(tiles_i[:], pattern=[[1, NT]], base=0, channel_multiplier=0).then_inc(consts, 1)
            g.iota(low_i[:], pattern=[[1, E], [-1, E]], base=0, channel_multiplier=0).then_inc(consts, 1)
            g.iota(tok_ids[:], pattern=[[GT * P, NG], [1, GT]], base=0, channel_multiplier=GT).then_inc(pad_out, 1)

            def all_max(n, u):
                pool.wait_ge(wabs, n + 1)
                if not early(n, 2):
                    pool.wait_ge(wscale, n - 1)
                pool.sem_inc(pool_go, 1)
                g.partition_all_reduce(amr[:, u:u + 1], am[:, u:u + 1], P, RMAX).then_inc(wabs_all, 1)

            def low_half(e, n, kind):
                pool.wait_ge(whi, 2 * (n + 1))
                if kind == 0:
                    hi = w1s[:, dyn(e), 0].rearrange("p a m n -> p (a m n)")
                    lo = w1s[:, dyn(e), 1].rearrange("p a m n -> p (a m n)")
                    g.tensor_tensor(lo, stage[:, 0], hi, ALU.subtract).then_inc(wlo, 1)
                else:
                    hi = w2s[:, dyn(e), :, 0].rearrange("p a h c -> p (a h) c")
                    lo = w2s[:, dyn(e), :, 1].rearrange("p a h c -> p (a h) c")
                    g.tensor_tensor(lo, stage[:, 1].rearrange("p (h c) -> p h c", h=HC), hi,
                                    ALU.subtract).then_inc(wlo, 1)

            def q_fin(i, u):
                for f in range(CC):
                    pool.wait_ge(q_act, 2 * (CC * (2 * i + u) + f + 1))
                    pool.sem_inc(pool_go, 1)
                    g.tensor_scalar(qt[:, u, f], qt[:, u, f], 1.0, None, ALU.min).then_inc(q_min, 1)
                for f in range(CC):
                    pool.wait_ge(q_min, CC * (2 * i + u) + f + 1)
                    g.tensor_tensor(qt[:, u, f], qt[:, u, f], qrelu[:, f], ALU.add).then_inc(q_done, 1)

            staged(pool, NG, [(lambda i, u: low_half(i, 2 * i + u, u), 1), (lambda i, u: all_max(2 * i + u, u), 0),
                              (lambda i, u: None if last_group(i, u) else q_fin(i, u), 1)])
            pool.wait_ge(h_steps, 1)
            g.partition_all_reduce(b1maxr[:], b1max[:], P, RMAX).then_inc(b1_all, 1)

            def scatter(i, u):
                n = 2 * i + u
                pool.wait_ge(placed, n + 1)
                pool.wait_ge(row_data, 2 * (n + 1))
                pool.sem_inc(pool_go, 1)
                for j in range(GT):
                    for k in range(2):
                        g.indirect_dma_start(
                            out=scratch, out_offset=bass.IndirectOffsetOnAxis(ap=idx[:, u, k, j:j + 1], axis=0),
                            in_=rows[:, u, j], in_offset=None).then_inc(scattered[u], 16)

            def low_and_scatter(i, u):
                if last_group(i, u):
                    scatter(i, u)
                low_half(i + NG // 2, NG + 2 * i + u, u)
                if not last_group(i, u):
                    scatter(i, u)

            staged(pool, NG, [(lambda i, u: all_max(NG + 2 * i + u, u), 0), (low_and_scatter, 1)])

            for u in range(2):
                pool.wait_ge(x2_out[u], 8 * NG)

            def add_rows(i, u):
                j = RING * i + u
                for h in range(halves(j)):
                    n = granules(j) + h
                    pool.wait_ge(y_done, n + 1)
                    if not early(n, 1):
                        pool.wait_ge(added, 16 * n)
                    pool.sem_inc(pool_go, 1)
                    g.indirect_dma_start(
                        out=out, out_offset=bass.IndirectOffsetOnAxis(ap=meta[:, u, h, E:E + 1], axis=0),
                        in_=y[:, u % 2, h], in_offset=None, bounds_check=T - 1, oob_is_err=False,
                        compute_op=ALU.add).then_inc(added, 16)

            staged(pool, NT, [(add_rows, 0)], turn=RING, alike=PAIRS)
            pool.wait_ge(added, 16 * granules(NT))

        @block.scalar
        def _(act):
            a = nc.scalar

            def scale_piece(e, n, kind):
                act.wait_ge(wscale, n + 1)
                a.activation(stage[:, kind], stage[:, kind], ACT.Copy, scale=wsc[:, kind:kind + 1]).then_inc(whi, 1)

            def round_piece(e, n, kind):
                act.wait_ge(whi, 2 * n + 1)
                act.sem_inc(act_go, 1)
                if kind == 0:
                    a.activation(w1s[:, dyn(e), 0].rearrange("p a m n -> p (a m n)"), stage[:, 0], ACT.Copy).then_inc(whi, 1)
                else:
                    a.activation(w2s[:, dyn(e), :, 0].rearrange("p a h c -> p (a h) c"),
                                 stage[:, 1].rearrange("p (h c) -> p h c", h=HC), ACT.Copy).then_inc(whi, 1)

            def zt_copy(i, u):
                g = 2 * i + u
                act.wait_ge(zt_psum, g + 1)
                if not early(i, 1):
                    act.wait_ge(kv_sum, GT * (g - 1))
                a.activation(zT[:, u], ps[:, 0:CC], ACT.Copy).then_inc(zt_sb, 1)

            def k_tile(i, u, j):
                n = GT * (2 * i + u) + j
                act.wait_ge(kv_biased, n + 1)
                if not early(n, 2):
                    act.wait_ge(k_done, n - 1)
                kin = kv[:, j, 0:NH, 0:D]
                a.activation(kexp[:, j % 2].rearrange("p (h d) -> p h d", h=NH), kin, ACT.Exp).then_inc(k_act, 1)
                if not early(n, GT):
                    act.wait_ge(kv_sum, n - GT + 1)
                a.activation(kf[:, j].rearrange("p (h d) -> p h d", h=NH), kin, ACT.Relu).then_inc(k_act, 1)

            def q_chunk(i, u, f):
                g = 2 * i + u
                if f == 0 and not early(i, 1):
                    act.wait_ge(qt_out[u], 16 * i)
                act.wait_ge(q_psum, CC * g + f + 1)
                a.activation(qt[:, u, f], ps[:, 6 + f], ACT.Exp, bias=bq_sb[:, f:f + 1]).then_inc(q_act, 1)
                if not early(g, 1):
                    act.wait_ge(q_done, CC * (g - 1) + f + 1)
                a.activation(qrelu[:, f], ps[:, 6 + f], ACT.Relu, bias=bq_sb[:, f:f + 1]).then_inc(q_act, 1)

            def kq_side(i, u):
                k_tile(i, u, 0)
                k_tile(i, u, 1)
                scale_piece(i, 2 * i + u, u)
                k_tile(i, u, 2)
                round_piece(i, 2 * i + u, u)
                k_tile(i, u, 3)
                q_chunk(i, u, 0)

            act.wait_ge(consts, NCONST)
            a.activation(qrelu[:, 0, 0:P], ident[:], ACT.Exp)
            act.wait_ge(params_in, 16 * NPARAM)
            staged(act, NG, [(kq_side, 1), (zt_copy, 0), (lambda i, u: q_chunk(i, u, 1), 1)])

            def normalise2(i, u):
                g = 2 * i + u
                act.wait_ge(rstd2, (RSTEPS + 1) * (g + 1))
                if not early(i, 1):
                    act.wait_ge(scattered[u], 16 * 2 * GT * i)
                for j in range(GT):
                    a.activation(rows[:, u, j, 0:C].bitcast(F32), x2[:, u, j], ACT.Identity,
                                 bias=shift[:, j:j + 1], scale=rstd[:, j:j + 1]).then_inc(z2_done, 1)

            def z2t_copy(i, u):
                g = 2 * i + u
                act.wait_ge(z2t_psum, g + 1)
                if not early(i, 1):
                    act.wait_ge(logit_psum, g - 1)
                a.activation(zT[:, u], ps[:, 0:CC], ACT.Copy).then_inc(z2t_sb, 1)

            def gap(i, u):
                act.wait_ge(gate_steps, GS * (2 * i + u) + GAP_AT)
                a.activation(wts[:, 1], wts[:, 0], ACT.Exp, scale=1.0 / ZSCALE).then_inc(gap_exp, 1)

            def w_square(i, u):
                n = NG + 2 * i + u
                e = i + NG // 2
                act.wait_ge(w_in[u], 16 * (e + 1))
                act.wait_ge(wscale, n - 1)
                act.sem_inc(act_go, 1)
                if u == 0:
                    a.activation(w1s[:, dyn(e), 0].rearrange("p a m n -> p (a m n)").bitcast(BF16), stage[:, 0],
                                 ACT.Square, scale=SQ, accum_out=am[:, 0:1]).then_inc(wabs, 1)
                else:
                    a.activation(w2s[:, dyn(e), :, 0].rearrange("p a h c -> p (a h) c").bitcast(BF16),
                                 stage[:, 1].rearrange("p (h c) -> p h c", h=HC),
                                 ACT.Square, scale=SQ, accum_out=am[:, 1:2]).then_inc(wabs, 1)

            staged(act, NG, [(normalise2, 1), (z2t_copy, 1),
                             (lambda i, u: scale_piece(i + NG // 2, NG + 2 * i + u, u), 1),
                             (lambda i, u: round_piece(i + NG // 2, NG + 2 * i + u, u), 1),
                             (w_square, 0), (gap, 1)])

            def hi_part(i, u):
                j = RING * i + u
                W = halves(j) * P
                for k in range(4):
                    act.wait_ge(hx_done, 4 * j + k + 1)
                    if k == 0 and not early(j, 2):
                        act.wait_ge(l2_psum, j - 1)
                    a.activation(hhi[:, u % 2, 2 * k:2 * k + 2, 0:W], hx[:, k, :, 0:W], ACT.Relu).then_inc(hi_done, 1)

            def zin_copy(i, u):
                j = RING * i + u
                W = halves(j) * P
                act.wait_ge(zin_psum, j + 1)
                if not early(j, 2):
                    act.wait_ge(l1_psum, 4 * (j - 1))
                a.activation(zin[:, u % 2, :, 0:W],
                             ps[:, 6 + u % 2].bitcast(F16).rearrange("p (c n) -> p c n", n=TS)[:, :, 0:W],
                             ACT.Copy).then_inc(zin_sb, 1)

            def split_hi(i, u):
                j = RING * i + u
                H = halves(j)
                act.wait_ge(rows_in[u], 16 * (i + 1))
                if not early(j, 2):
                    act.wait_ge(zin_psum, j - 1)
                a.activation(zsplit[:, u % 2, 0:H, 0:C], rin[:, u, 0:H, 0:C].bitcast(F32), ACT.Copy).then_inc(zhi, 1)

            def meta_copy(i, u):
                j = RING * i + u
                H = halves(j)
                act.wait_ge(rows_in[u], 16 * (i + 1))
                if not early(i, 1):
                    act.wait_ge(added, 16 * granules(j - RING + 1))
                a.activation(meta[:, u, 0:H, E:E + 1], rin[:, u, 0:H, TOK:TOK + 1], ACT.Copy).then_inc(meta_done, 1)
                a.activation(meta[:, u, 0:H, 0:E].bitcast(F32), rin[:, u, 0:H, COMB:COMB + E].bitcast(F32),
                             ACT.Copy).then_inc(meta_done, 1)

            def weigh(i, u):
                j = RING * i + u
                e = expert_of(act, "act", j)
                act.wait_ge(meta_done, 2 * (j + 1))
                if not early(j, 2):
                    act.wait_ge(added, 16 * granules(j - 1))
                for h in range(halves(j)):
                    act.wait_ge(yv_done, granules(j) + h + 1)
                    a.activation(y[:, u % 2, h], yv[:, h], ACT.Copy,
                                 scale=meta[:, u, h].bitcast(F32)[:, dyn(e)]).then_inc(y_done, 1)

            act.wait_ge(tables, 1)
            act.wait_ge(num_psum, GT * NG)
            for j in range(PAIRS, NT):
                expert_of(act, "act", j)
            staged(act, NT, [(split_hi, 0), (hi_part, 1), (zin_copy, 0), (meta_copy, 0), (weigh, 2)], turn=RING, alike=PAIRS)

        @block.vector
        def _(dve):
            v = nc.vector

            def chain(semaphore, base, on=True):
                count = [0]

                def step(op, *args):
                    if on:
                        if count[0]:
                            dve.wait_ge(semaphore, base + count[0])
                        op(*args).then_inc(semaphore, 1)
                        count[0] += 1
                return step, count

            v.memset(pad[:], 0).then_inc(pad_out, 1)
            v.memset(kv_bd[:], 0.0).then_inc(kv_ones, 1)
            dve.wait_ge(pad_out, 2)
            v.memset(pad[:, TOK:TOK + 1], T).then_inc(pad_out, 1)
            dve.wait_ge(consts, NCONST)

            def w_abs(n, kind, i):
                dve.wait_ge(w_in[kind], 16 * (i + 1))
                if not early(n, 2):
                    dve.wait_ge(wabs_all, n - 1)
                v.tensor_reduce(am[:, kind:kind + 1], stage[:, kind], AX.X, ALU.max,
                                apply_absolute_value=True).then_inc(wabs, 1)

            def w_scale(w, e, n, kind, k, squares=False):
                col = slice(kind, kind + 1)
                low_bits = 24 if squares else 23
                back = 2.0 ** 65 / SQ / TOP if squares else 1.0 / TOP
                if k == 0:
                    dve.wait_ge(wabs_all, n + 1)
                    w(v.tensor_scalar, wt[:, col], amr[:, col], (TINY * SQ) ** 2 if squares else TINY, None, ALU.max)
                elif k == 1:
                    w(v.tensor_scalar, wt[:, col].bitcast(I32), wt[:, col].bitcast(I32), low_bits, 23,
                      ALU.logical_shift_right, ALU.logical_shift_left)
                elif k == 2:
                    w(v.tensor_scalar, winv[:, dyn(e), kind], wt[:, col], back, None, ALU.mult)
                elif k == 3:
                    w(v.tensor_scalar, am[:, col], wt[:, col], back, None, ALU.mult)
                else:
                    dve.wait_ge(wscale_s, 4 * (n + 1))
                    if not early(n, 2):
                        dve.wait_ge(whi, 2 * (n - 1))
                    v.reciprocal(wsc[:, col], am[:, col]).then_inc(wscale, 1)

            def statistics(src, j, done):
                v.bn_stats(st[:, j], src[:, j]).then_inc(done, 1)

            def aggregates(n, stats, done):
                dve.wait_ge(stats, GT * (n + 1))
                dve.sem_inc(dve_go, 1)
                for j in range(GT):
                    v.bn_aggr(mv[:, j], st[:, j]).then_inc(done, 1)

            def root(r, k, scale):
                if k == 0:
                    r(v.tensor_scalar, ve[:], mv[:, :, 1], LN_EPS, 1.0 / scale ** 2, ALU.add, ALU.mult)
                elif k == 1:
                    r(v.tensor_scalar, half[:], ve[:].bitcast(I32), 1, None, ALU.logical_shift_right)
                elif k == 2:
                    r(v.tensor_scalar, rstd[:].bitcast(I32), half[:], -1.0, float(0x5F3759DF), ALU.mult, ALU.add)
                elif k % 3 == 0:
                    r(v.tensor_tensor, nt[:, 0], rstd[:], ve[:], ALU.mult)
                elif k % 3 == 1:
                    r(v.scalar_tensor_tensor, nt[:, 1], nt[:, 0], -0.5, rstd[:], ALU.mult, ALU.mult)
                else:
                    r(v.scalar_tensor_tensor, rstd[:], nt[:, 1], 1.5, rstd[:], ALU.add, ALU.mult)

            def normalise(dst, src, j, done):
                v.tensor_scalar(dst[:, j], src[:, j], mv[:, j, 0:1], rstd[:, j:j + 1],
                                ALU.subtract, ALU.mult).then_inc(done, 1)

            def slot1(i, u, norm=True, kv_on=True):
                g = 2 * i + u
                ib, ub = (i, 0) if u else (i - 1, 1)
                b = g - 1
                r, _ = chain(rstd1, RSTEPS * g, norm)
                w, _ = chain(wscale_s, 4 * b, kv_on)

                def bias(j):
                    if kv_on:
                        n = GT * b + j
                        dve.wait_ge(kv_psum, n + 1)
                        if not early(b, 1):
                            dve.wait_ge(kv_sum, n - GT + 1)
                        v.tensor_tensor(kv[:, j, :, 0:D], ps[:, 4 + j % 2].rearrange("p (h d) -> p h d", d=D),
                                        bkv_sb[:], ALU.add).then_inc(kv_biased, 1)

                def k_fin(j):
                    if kv_on:
                        dve.wait_ge(k_act, 2 * (GT * b + j + 1))
                        v.scalar_tensor_tensor(kf[:, j], kexp[:, j % 2], 1.0, kf[:, j],
                                               ALU.min, ALU.add).then_inc(k_done, 1)

                if norm:
                    dve.wait_ge(x_in[u], 16 * (i + 1))
                    for j in range(GT):
                        statistics(xr[:, u], j, stats1)
                    if not early(g, 1):
                        dve.wait_ge(z1, GT * g)
                    aggregates(g, stats1, aggr1)
                bias(0)
                if norm:
                    dve.wait_ge(aggr1, GT * (g + 1))
                for k in range(4):
                    root(r, k, 1.0)
                    if kv_on:
                        w_scale(w, ib, b, ub, k)
                k_fin(0)
                bias(1)
                if kv_on:
                    w_scale(w, ib, b, ub, 4)
                for k in range(4, 7):
                    root(r, k, 1.0)
                bias(2)
                k_fin(1)
                for k in range(7, RSTEPS):
                    root(r, k, 1.0)
                if norm:
                    dve.wait_ge(rstd1, RSTEPS * (g + 1))
                    if not early(g, 1):
                        dve.wait_ge(zt_psum, g)
                    normalise(z, xr[:, u], 0, z1)
                    normalise(z, xr[:, u], 1, z1)
                bias(3)
                k_fin(2)
                if norm:
                    normalise(z, xr[:, u], 2, z1)
                    normalise(z, xr[:, u], 3, z1)
                k_fin(3)
                if norm:
                    w_abs(g, u, i)

            v.memset(ends[:], 0.0)
            v.memset(origin[:], float(E * CAP))
            v.tensor_copy(ident16[:], ident[:])
            v.tensor_copy(rev[:], rev_i[:])
            v.tensor_copy(base[:], base_i[:])
            v.tensor_copy(start_row[:], base_i[:])
            v.tensor_copy(tile_no[:], tiles_i[:])
            v.tensor_scalar(low[:], low_i[:], 0, None, ALU.is_ge)
            slot1(0, 0, kv_on=False)
            dve.wait_ge(params_in, 16 * NPARAM)
            dve.wait_ge(kv_ones, 2)
            v.tensor_reduce(b1max[:], b1_sb[:], AX.X, ALU.max, apply_absolute_value=True).then_inc(h_steps, 1)
            for k in range(1, 4):
                slot1(k // 2, k % 2)
            with dve.Fori(2, NG // 2) as i:
                slot1(i, 0)
                slot1(i, 1)
            slot1(NG // 2, 0, norm=False)

            dve.wait_ge(kv_sum, GT * NG)
            for f in range(CC):
                for h in range(HB):
                    v.tensor_copy(kv_bd[h * D:(h + 1) * D, f, h * VW:(h + 1) * VW],
                                  ps[h * D:(h + 1) * D, 2 + f, h * VW:(h + 1) * VW]).then_inc(kvbd, 1)

            for f in range(CC):
                dve.wait_ge(q_act, 2 * (CC * (NG - 1) + f + 1))
                if f == 0:
                    dve.wait_ge(q_done, CC * (NG - 1))
                v.scalar_tensor_tensor(qt[:, (NG - 1) % 2, f], qt[:, (NG - 1) % 2, f], 1.0, qrelu[:, f],
                                       ALU.min, ALU.add).then_inc(q_done, 1)

            v.memset(msum[:].bitcast(I32), 0).then_inc(kv_ones, 1)
            v.memset(rows[:, :, :, TOK + 1:ROW].rearrange("p b j w -> p (b j) w"), 0).then_inc(kv_ones, 1)
            dve.wait_ge(kv_ones, 4)

            def wide(ap):
                return ap.unsqueeze(2).broadcast_to([P, GT, E])

            def slot2(i, u, attend=True, gate=True):
                g = 2 * i + u
                ib, ub = (i, 0) if u else (i - 1, 1)
                b = g - 1
                r, _ = chain(rstd2, (RSTEPS + 1) * g, attend)
                c, count = chain(gate_steps, GS * b, gate)
                w, _ = chain(wscale_s, 4 * (NG + g), attend)
                lg = ps[:, 2, 0:GT * E].rearrange("p (j e) -> p j e", e=E)
                m1, m2 = chosen[:, 0], chosen[:, 1]
                nd = ps[:, 4:4 + GT, 0:NH * VW].rearrange("p j (h w) -> p j h w", w=VW)

                def divide(j):
                    if attend:
                        v.tensor_tensor(x2[:, u, j].rearrange("p (h d) -> p h d", d=D), nd[:, j, :, 0:D],
                                        rden[:, j].unsqueeze(2).broadcast_to([P, NH, D]), ALU.mult).then_inc(att, 1)

                if attend:
                    if not early(g, 1):
                        dve.wait_ge(att, GT * g)
                    dve.wait_ge(num_psum, GT * (g + 1))
                    v.tensor_scalar(den[:], nd[:, :, :, D], ATT_EPS, None, ALU.add).then_inc(dens, 1)
                    dve.wait_ge(dens, g + 1)
                    v.reciprocal(rden[:], den[:]).then_inc(rdens, 1)
                    if not early(i, 1):
                        dve.wait_ge(x2_out[u], 16 * i)
                    dve.wait_ge(rdens, g + 1)
                for j in range(GT):
                    divide(j)
                if attend:
                    dve.wait_ge(att, GT * (g + 1))
                    dve.wait_ge(x_in[u], 16 * (NG // 2 + i + 1))
                    v.tensor_tensor(x2[:, u], x2[:, u], xr[:, u], ALU.add).then_inc(x2_done, 1)
                if attend:
                    dve.wait_ge(x2_done, g + 1)
                    for j in range(GT):
                        statistics(x2[:, u], j, stats2)
                    if not early(g, 1):
                        dve.wait_ge(z2_done, GT * g)
                    aggregates(g, stats2, aggr2)
                    dve.wait_ge(aggr2, GT * (g + 1))
                for k in range(4):
                    root(r, k, ZSCALE)
                if gate:
                    dve.wait_ge(logit_psum, b + 1)
                    v.tensor_copy(rows[:, ub, :, TOK], tok_ids[:, dyn(b)].rearrange("p a j -> p (a j)")).then_inc(row_data, 1)
                c(v.tensor_reduce, mx[:, 0], lg, AX.X, ALU.max)
                root(r, 4, ZSCALE)
                c(v.tensor_tensor, eq[:], lg, wide(mx[:, 0]), ALU.is_equal)
                root(r, 5, ZSCALE)
                c(v.tensor_tensor, cand[:], eq[:], rev[:], ALU.mult)
                root(r, 6, ZSCALE)
                c(v.tensor_reduce, first[:], cand[:], AX.X, ALU.max)
                root(r, 7, ZSCALE)
                c(v.tensor_tensor, m1, cand[:], wide(first[:]), ALU.is_equal)
                root(r, 8, ZSCALE)
                c(v.scalar_tensor_tensor, lg2[:], m1, -3.0e38, lg, ALU.mult, ALU.add)
                root(r, 9, ZSCALE)
                c(v.tensor_reduce, mx[:, 1], lg2[:], AX.X, ALU.max)
                root(r, 10, ZSCALE)
                c(v.tensor_tensor, eq[:], lg2[:], wide(mx[:, 1]), ALU.is_equal)
                root(r, 11, ZSCALE)
                c(v.tensor_tensor, cand[:], eq[:], rev[:], ALU.mult)
                r(v.scalar_tensor_tensor, shift[:], mv[:, :, 0], -1.0, rstd[:], ALU.mult, ALU.mult)
                c(v.tensor_reduce, first[:], cand[:], AX.X, ALU.max)
                c(v.tensor_tensor, wts[:, 0], mx[:, 1], mx[:, 0], ALU.subtract)
                assert count[0] in (0, GAP_AT)
                if attend:
                    w_scale(w, i + NG // 2, NG + g, u, 0, squares=True)
                c(v.tensor_tensor, m2, cand[:], wide(first[:]), ALU.is_equal)
                if attend:
                    w_scale(w, i + NG // 2, NG + g, u, 1, squares=True)
                c(v.tensor_tensor, msum[:, 0:GT], m1, m2, ALU.add)
                if attend:
                    w_scale(w, i + NG // 2, NG + g, u, 2, squares=True)
                if gate:
                    dve.wait_ge(gap_exp, b + 1)
                c(v.tensor_scalar, wts[:, 2], wts[:, 1], 1.0, None, ALU.add)
                if attend:
                    w_scale(w, i + NG // 2, NG + g, u, 3, squares=True)
                c(v.reciprocal, wts[:, 3], wts[:, 2])
                if attend:
                    w_scale(w, i + NG // 2, NG + g, u, 4, squares=True)
                c(v.tensor_tensor, wts[:, 4], wts[:, 1], wts[:, 3], ALU.mult)
                if not gate:
                    return
                c(v.tensor_tensor, cb[:], chosen[:], wts[:, 3:5].unsqueeze(3).broadcast_to([P, 2, GT, E]), ALU.mult)
                dve.wait_ge(rank_psum, b + 1)
                ranks = ps[:, 3, 0:(GT + 1) * E].rearrange("p (j e) -> p j e", e=E)
                c(v.tensor_tensor, pos[:], ranks[:, 0:GT], base[:].unsqueeze(1).broadcast_to([P, GT, E]), ALU.add)
                v.tensor_tensor(rows[:, ub].bitcast(F32)[:, :, COMB:COMB + E], cb[:, 0], cb[:, 1],
                                ALU.add).then_inc(row_data, 1)
                c(v.tensor_tensor, base[:], base[:], ranks[:, GT], ALU.add)
                assert count[0] == GS
                v.tensor_tensor(pos2[:], chosen[:], pos[:].unsqueeze(1).broadcast_to([P, 2, GT, E]),
                                ALU.mult).then_inc(pl_steps, 1)
                if not early(ib, 1):
                    dve.wait_ge(scattered[ub], 16 * 2 * GT * ib)
                dve.wait_ge(pl_steps, b + 1)
                v.tensor_reduce(idx[:, ub], pos2[:], AX.X, ALU.add).then_inc(placed, 1)
                dve.wait_ge(gate_steps, GS * (b + 1))

            for k in range(4):
                slot2(k // 2, k % 2, gate=k > 0)
            with dve.Fori(2, NG // 2) as i:
                slot2(i, 0)
                slot2(i, 1)

            dve.wait_ge(q_done, CC * NG)
            for kind in range(2):
                v.memset(past[kind][:], 0.0)

            dve.wait_ge(b1_all, 1)
            dve.wait_ge(wscale, 2 * NG)
            step, _ = chain(h_scales, 0)
            step(v.scalar_tensor_tensor, htmp[:, 0], winv[:, :, 0], 2 * TOP * float(C) ** 0.5 * ZBOUND, b1maxr[:],
                 ALU.mult, ALU.add)
            step(v.tensor_scalar, htmp[:, 1].bitcast(I32), htmp[:, 0].bitcast(I32), 23, 23,
                                 ALU.logical_shift_right, ALU.logical_shift_left)
            step(v.tensor_scalar, hinv[:], htmp[:, 1], 1.0 / TOP, None, ALU.mult)
            step(v.reciprocal, hscale[:], hinv[:])
            step(v.scalar_tensor_tensor, l1_scale[:], hscale[:], 1.0 / ZSCALE, winv[:, :, 0], ALU.mult, ALU.mult)
            step(v.tensor_tensor, y_scale[:], hinv[:], winv[:, :, 1], ALU.mult)
            step(v.tensor_tensor, b1s[:], b1_sb[:], hscale[:].unsqueeze(2).broadcast_to([P, E, HC]), ALU.mult)
            slot2(NG // 2, 0, attend=False)

            step, count = chain(tab_steps, 0)
            step(v.tensor_copy, pad_row[:], base[0:1])
            step(v.tensor_tensor, counts[:, 0], base[0:1], start_row[0:1], ALU.subtract)
            step(v.tensor_scalar, cnt_i[:, 0], counts[:, 0], float(P - 1), None, ALU.add)
            step(v.tensor_scalar, cnt_i[:, 1], cnt_i[:, 0], P.bit_length() - 1, None, ALU.logical_shift_right)
            step(v.tensor_scalar, cnt_i[:, 2], cnt_i[:, 0], TS.bit_length() - 1, None, ALU.logical_shift_right)
            step(v.tensor_copy, counts[:, 1:3], cnt_i[:, 1:3])
            step(v.tensor_tensor, ends3[:], low[:], counts[:, 2].unsqueeze(1).broadcast_to([1, E, E]), ALU.mult)
            step(v.tensor_reduce, ends[:, 0, 1:], ends3[:], AX.X, ALU.add)
            step(v.tensor_scalar, ends[:, 0, 1:], ends[:, 0, 1:], float(PAIRS), None, ALU.min)
            step(v.tensor_tensor, counts[:, 3], ends[:, 0, 1:], ends[:, 0, 0:E], ALU.subtract)
            step(v.scalar_tensor_tensor, nsingle[:], counts[:, 3], -2.0, counts[:, 1], ALU.mult, ALU.add)
            step(v.tensor_tensor, ends3[:], low[:], nsingle[:].unsqueeze(1).broadcast_to([1, E, E]), ALU.mult)
            step(v.tensor_reduce, ends[:, 1, 1:], ends3[:], AX.X, ALU.add)
            step(v.scalar_tensor_tensor, origin[:, 0, 0:E], ends[:, 0, 0:E], -float(TS), start_row[0:1], ALU.mult, ALU.add)
            step(v.scalar_tensor_tensor, origin[:, 1, 0:E], counts[:, 3], float(TS), start_row[0:1], ALU.mult, ALU.add)
            step(v.scalar_tensor_tensor, origin[:, 1, 0:E], ends[:, 1, 0:E], -float(P), origin[:, 1, 0:E], ALU.mult, ALU.add)
            dve.wait_ge(tab_steps, count[0])
            kinds = []
            for kind, semaphore in ((0, tab_p), (1, tab_s)):
                n = (PAIRS, SINGLES)[kind]
                kinds.append((kind, n, slice(kind * PAIRS, kind * PAIRS + n), chain(semaphore, 0)[0]))
            for kind, n, _, step in kinds:
                step(v.tensor_tensor, past[kind][:, :, 0:E + 1], tile_no[:, 0:n].unsqueeze(2).broadcast_to([1, n, E + 1]),
                     ends[:, kind].unsqueeze(1).broadcast_to([1, n, E + 1]), ALU.is_ge)
            for kind, n, _, step in kinds:
                step(v.tensor_reduce, where[kind][:, 0], past[kind][:, :, 1:E + 1], AX.X, ALU.add)
            for kind, n, _, step in kinds:
                step(v.tensor_tensor, here[kind][:], past[kind][:, :, 0:E + 1], past[kind][:, :, 1:E + 2], ALU.subtract)
            for kind, n, _, step in kinds:
                step(v.tensor_tensor, here[kind][:], here[kind][:],
                     origin[:, kind].unsqueeze(1).broadcast_to([1, n, E + 1]), ALU.mult)
            for kind, n, _, step in kinds:
                step(v.tensor_reduce, where[kind][:, 1], here[kind][:], AX.X, ALU.add)
            for kind, n, _, step in kinds:
                step(v.scalar_tensor_tensor, where[kind][:, 1], tile_no[:, 0:n], float((TS, P)[kind]), where[kind][:, 1],
                     ALU.mult, ALU.add)
            for kind, n, tiles, step in kinds:
                step(v.tensor_scalar, tile_row[:, tiles], where[kind][:, 1], float(E * CAP), None, ALU.min)
            for kind, n, tiles, step in kinds:
                step(v.tensor_scalar, tile_exp[:, tiles], where[kind][:, 0], float(E - 1), None, ALU.min)
            dve.wait_ge(tab_p, 8)
            dve.wait_ge(tab_s, 8)
            v.memset(htmp[:], 0.0).then_inc(tables, 1)

            def y_part(i, u, h, e):
                j = RING * i + u
                n = granules(j) + h
                if h == 0:
                    dve.wait_ge(l2_psum, j + 1)
                if not early(j, 1):
                    dve.wait_ge(y_done, granules(j - 1) + h + 1)
                v.scalar_tensor_tensor(yu[:, h], ps[:, 4 + h, 0:C], y_scale[:, dyn(e)],
                                       b2_sb[:, dyn(e)].rearrange("p a c -> p (a c)"), ALU.mult, ALU.add).then_inc(yu_done, 1)
                dve.wait_ge(yu_done, n + 1)
                v.scalar_tensor_tensor(yv[:, h], ps[:, 4 + h, C:2 * C], y_scale[:, dyn(e)], yu[:, h],
                                       ALU.mult, ALU.add).then_inc(yv_done, 1)

            def hidden(i, u):
                j = RING * i + u
                W = halves(j) * P
                e = expert_of(dve, "dve", j)

                def scaled(k):
                    dve.wait_ge(l1_psum, 4 * j + k + 1)
                    if not early(j, 1):
                        dve.wait_ge(lo_done, 4 * (j - 1) + k + 1)
                    v.scalar_tensor_tensor(
                        hx[:, k, :, 0:W], ps[:, k].rearrange("p (h n) -> p h n", h=2)[:, :, 0:W], l1_scale[:, dyn(e)],
                        b1s[:, dyn(e), 2 * k:2 * k + 2].rearrange("p a h -> p (a h)").unsqueeze(2).broadcast_to([P, 2, W]),
                        ALU.mult, ALU.add).then_inc(hx_done, 1)

                def lo_part(k):
                    dve.wait_ge(hi_done, 4 * j + k + 1)
                    v.scalar_tensor_tensor(hlo[:, u % 2, 2 * k:2 * k + 2, 0:W], hx[:, k, :, 0:W], 0.0,
                                           hhi[:, u % 2, 2 * k:2 * k + 2, 0:W], ALU.max, ALU.subtract).then_inc(lo_done, 1)

                if not early(j, 2):
                    dve.wait_ge(l2_psum, j - 1)
                scaled(0)
                scaled(1)
                lo_part(0)
                scaled(2)
                lo_part(1)
                scaled(3)
                lo_part(2)
                lo_part(3)

            def split_lo(i, u):
                j = RING * i + u
                H = halves(j)
                dve.wait_ge(zhi, j + 1)
                v.tensor_tensor(zsplit[:, u % 2, 0:H, C:2 * C], rin[:, u, 0:H, 0:C].bitcast(F32),
                                zsplit[:, u % 2, 0:H, 0:C], ALU.subtract).then_inc(zlo, 1)

            def result(i, u):
                e = expert_of(dve, "dve", RING * i + u)
                if early(RING * i + u, 1):
                    dve.wait_ge(b2_in, 16)
                for h in range(halves(RING * i + u)):
                    y_part(i, u, h, e)

            dve.wait_ge(tables, 1)
            for j in range(PAIRS, NT):
                expert_of(dve, "dve", j)
            dve.wait_ge(wlo, 2 * NG)
            for u in range(2):
                dve.wait_ge(scattered[u], 16 * GT * NG)
            for u in range(2):
                dve.wait_ge(x2_out[u], 8 * NG)
            staged(dve, NT, [(split_lo, 0), (hidden, 1), (result, 2)], turn=RING, alike=PAIRS)

        @block.tensor
        def _(pe):
            t = nc.tensor
            pe.wait_ge(consts, NCONST)

            def keep_warm(rhs, bank, number):
                for _ in range(number):
                    t.matmul(ps[:, bank, 0:rhs.shape[-1]], tri[:], rhs, start=True, stop=True)

            with pe.Fori(0, 8):
                keep_warm(ones[:], 7, 8)

            def turn(src, i, u, ready, psum_read, done):
                g = 2 * i + u
                if not early(g, 1):
                    pe.wait_ge(psum_read, g)
                for j in range(GT):
                    pe.wait_ge(ready, GT * g + j + 1)
                    for c in range(CC):
                        ins = t.transpose(ps[:, c, j * P:(j + 1) * P], src[:, j, c * P:(c + 1) * P], ident[:])
                ins.then_inc(done, 1)

            def project(i, u, part):
                g = 2 * i + u
                if early(g, 1):
                    pe.wait_ge(params_in, 16 * NPARAM)
                if part == 0:
                    pe.wait_ge(zt_sb, g + 1)
                head = early(g, 1)
                tail = isinstance(g, int) and g == NG - 1

                def proj(j):
                    n = GT * g + j
                    if not early(n, 2):
                        pe.wait_ge(kv_biased, n - 1)
                    for c in range(CC):
                        ins = t.matmul(ps[:, 4 + j % 2], zT[:, u, c, j * P:(j + 1) * P],
                                       wkv_sb[:, c].rearrange("p k n -> p (k n)"), start=(c == 0), stop=(c == CC - 1))
                    ins.then_inc(kv_psum, 1)

                def add_kv(j):
                    pe.wait_ge(k_done, GT * g + j + 1)
                    for f in range(CC):
                        ins = t.matmul(ps[:, 2 + f, 0:NHC], kf[:, j, f * P:(f + 1) * P],
                                       kv[:, j, NH + f * HB:NH + (f + 1) * HB].rearrange("p h w -> p (h w)"),
                                       start=(head and j == 0), stop=(tail and j == GT - 1))
                    ins.then_inc(kv_sum, 1)

                def q_chunk(f):
                    if not head:
                        pe.wait_ge(q_act, 2 * (CC * (g - 1) + f + 1))
                    for c in range(CC):
                        ins = t.matmul(ps[:, 6 + f], wq_sb[:, c, f * P:(f + 1) * P], zT[:, u, c],
                                       start=(c == 0), stop=(c == CC - 1))
                    ins.then_inc(q_psum, 1)

                if part == 0:
                    proj(0)
                    proj(1)
                    proj(2)
                    add_kv(0)
                    proj(3)
                    add_kv(1)
                    q_chunk(0)
                    add_kv(2)
                else:
                    add_kv(3)
                    q_chunk(1)

            staged(pe, NG, [(lambda i, u: project(i, u, 0), 1), (lambda i, u: turn(z, i, u, z1, zt_sb, zt_psum), 0),
                            (lambda i, u: project(i, u, 1), 1)])

            pe.wait_ge(kvbd, CC * HB)
            pe.wait_ge(q_act, 2 * CC * NG)

            def numerators(i, u):
                g = 2 * i + u
                pe.wait_ge(qt_in[u], 16 * (i + 1))
                for j in range(GT):
                    if not early(g, 1):
                        pe.wait_ge(att, GT * (g - 1) + j + 1)
                    for f in range(CC):
                        ins = t.matmul(ps[:, 4 + j, f * NHC:(f + 1) * NHC], qt[:, u, f, j * P:(j + 1) * P],
                                       kv_bd[:, f], start=True, stop=True)
                    ins.then_inc(num_psum, 1)

            def logits(i, u):
                g = 2 * i + u
                pe.wait_ge(z2t_sb, g + 1)
                if not early(g, 1):
                    pe.wait_ge(gate_steps, GS * (g - 1) + 6)
                for j in range(GT):
                    for c in range(CC):
                        ins = t.matmul(ps[:, 2, j * E:(j + 1) * E], zT[:, u, c, j * P:(j + 1) * P], gw_sb[:, c],
                                       start=(c == 0), stop=(c == CC - 1))
                ins.then_inc(logit_psum, 1)

            def rank(i, u):
                g = 2 * i + u
                pe.wait_ge(gate_steps, GS * g + GAP_AT + 2)
                t.matmul(ps[:, 3, 0:(GT + 1) * E], tri[:], msum[:].rearrange("p j e -> p (j e)"), start=True, stop=False)
                for j in range(GT):
                    ins = t.matmul(ps[:, 3, (j + 1) * E:(GT + 1) * E].rearrange("p (k e) -> p k e", e=E), ones[:],
                                   msum[:, j].unsqueeze(1).broadcast_to([P, GT - j, E]),
                                   start=False, stop=(j == GT - 1))
                ins.then_inc(rank_psum, 1)

            staged(pe, NG, [(lambda i, u: turn(rows[:, u].bitcast(F32), i, u, z2_done, z2t_sb, z2t_psum), 2), (logits, 2),
                            (numerators, 0), (rank, 2)])

            pe.wait_ge(tables, 1)
            for j in range(PAIRS, NT):
                expert_of(pe, "pe", j)
            keep_warm(w1s[:, 0, 0, 0:4].rearrange("p m n -> p (m n)"), 7, 9)

            def layer1(i, u):
                j = RING * i + u
                W = halves(j) * P
                e = expert_of(pe, "pe", j)
                if early(j, 1):
                    pe.wait_ge(wlo, 2 * NG)
                pe.wait_ge(zin_sb, j + 1)
                for k in range(4):
                    if not early(j, 1):
                        pe.wait_ge(hx_done, 4 * (j - 1) + k + 1)
                    for h in range(2):
                        n = 0
                        for c in range(CC):
                            whi_ap, wlo_ap = (w1s[:, dyn(e), part, c * HC + 2 * k + h].rearrange("p a n -> p (a n)")
                                              for part in range(2))
                            for w, zz in ((whi_ap, c), (whi_ap, CC + c), (wlo_ap, c)):
                                ins = t.matmul(ps[:, k, h * TS:h * TS + W], w, zin[:, u % 2, zz, 0:W],
                                               start=(n == 0), stop=(n == 3 * CC - 1))
                                n += 1
                    ins.then_inc(l1_psum, 1)

            def layer2(i, u):
                j = RING * i + u
                e = expert_of(pe, "pe", j)
                if not early(j, 1):
                    pe.wait_ge(yv_done, granules(j))
                for c in range(HC):
                    if c % 2 == 0:
                        pe.wait_ge(lo_done, 4 * j + c // 2 + 1)
                    both = w2s[:, dyn(e), c].rearrange("p a k n -> p (a k n)")
                    high = w2s[:, dyn(e), c, 0].rearrange("p a n -> p (a n)")
                    for h in range(halves(j)):
                        t.matmul(ps[:, 4 + h], hhi[:, u % 2, c, h * P:(h + 1) * P], both, start=(c == 0), stop=False)
                    for h in range(halves(j)):
                        ins = t.matmul(ps[:, 4 + h, C:2 * C], hlo[:, u % 2, c, h * P:(h + 1) * P], high,
                                       start=False, stop=(c == HC - 1))
                ins.then_inc(l2_psum, 1)

            def turn_rows(i, u):
                pe.wait_ge(zlo, RING * i + u + 1)
                j = RING * i + u
                if not early(j, 2):
                    pe.wait_ge(zin_sb, RING * i + u - 1)
                for c in range(2 * CC):
                    for h in range(halves(j)):
                        ins = t.transpose(ps[:, 6 + u % 2].bitcast(F16)[:, c * TS + h * P:c * TS + (h + 1) * P],
                                          zsplit[:, u % 2, h, c * P:(c + 1) * P], ident16[:])
                ins.then_inc(zin_psum, 1)

            staged(pe, NT, [(layer1, 1), (turn_rows, 0), (layer2, 2)], turn=RING, alike=PAIRS)


def kernel(**inputs):
    import numpy as _np
    import concourse.bacc as _bacc
    from concourse import mybir as _mybir
    from concourse.bass_utils import run_bass_kernel_spmd as _run

    a = {k: _np.asarray(v) for k, v in inputs.items()}
    B, L, C = a["L0_attn_x"].shape
    E, HID, _ = a["L0_ffn_w1"].shape
    cc, hc = C // 128, HID // 128

    def rows_first(w):
        return w.reshape(cc, 128, -1).transpose(1, 0, 2)

    arrays = {
        "x": a["L0_attn_x"].reshape(B * L, C),
        "wq": rows_first(a["L0_attn_Wq"]), "bq": a["L0_attn_bq"].reshape(cc, 128).T,
        "wk": rows_first(a["L0_attn_Wk"]), "bk": a["L0_attn_bk"],
        "wv": rows_first(a["L0_attn_Wv"]), "bv": a["L0_attn_bv"],
        "gate_w": rows_first(a["L0_ffn_gate_w"].T),
        "w1": a["L0_ffn_w1"].reshape(E, HID, cc, 128).transpose(0, 3, 2, 1).reshape(E, 128, cc * HID),
        "b1": a["L0_ffn_b1"].reshape(E, hc, 128).transpose(2, 0, 1),
        "w2": a["L0_ffn_w2"].reshape(E, C, hc, 128).transpose(0, 3, 2, 1).reshape(E, 128, hc * C),
        "b2": a["L0_ffn_b2"].reshape(E * C),
    }
    arrays = {k: _np.ascontiguousarray(v) for k, v in arrays.items()}
    nc = _bacc.Bacc("TRN2", target_bir_lowering=False, num_devices=1)
    args = [nc.dram_tensor(k, v.shape, _mybir.dt.from_np(v.dtype), kind="ExternalInput").ap()
            for k, v in arrays.items()]
    out = nc.dram_tensor("out", (B * L, C), _mybir.dt.float32, kind="ExternalOutput").ap()
    attention_moe(nc, *args, out)
    r = _run(nc, [arrays], core_ids=[0])
    return r.results[0]["out"].reshape(B, L, C)
```
